# Optimizing a Trainium2 kernel written in Bass

```python
import numpy as np
import jax
import jax.numpy as jnp

def _softmax(x, axis=-1):
    return jax.nn.softmax(x, axis=axis)

def _gelu(x):
    return jax.nn.gelu(x, approximate=True)

def _silu(x):
    return jax.nn.silu(x)

def _sigmoid(x):
    return jax.nn.sigmoid(x)

def _layernorm(x, axis=-1, eps=1e-05):
    m = jnp.mean(x, axis=axis, keepdims=True)
    v = jnp.var(x, axis=axis, keepdims=True)
    return (x - m) / jnp.sqrt(v + eps)

def _scatter_add(tgt, idx, src, axis=0):
    return tgt.at[idx].add(src)

def _segment_sum(src, seg, n):
    return jax.ops.segment_sum(src, seg, n)
kernel_name = 'mk_adaln_d1_jaxref_r8_554dfc'

def setup_inputs(seed: int=0):
    np.random.seed(seed)
    _w = jnp.asarray

    def _L0_attn_setup():
        import jax, jax.numpy as jnp
        import numpy as np
        B, S, D = (2, 256, 128)
        H = 16
        HD = D // H

        def _rope_tables(seq_len, head_dim, dtype):
            pos = jnp.arange(seq_len, dtype=dtype)
            inv = jnp.power(10000.0, -2.0 * jnp.arange(head_dim // 2, dtype=dtype) / head_dim)
            ang = pos[:, None] * inv[None, :]
            cos_pos = jnp.repeat(jnp.cos(ang), 2, axis=-1)
            sin_pos = jnp.repeat(jnp.sin(ang), 2, axis=-1)
            return (cos_pos, sin_pos)

        def _rotate_half_interleaved(x):
            x2 = jnp.stack([-x[..., 1::2], x[..., 0::2]], axis=-1)
            return x2.reshape(x.shape)
        key = jax.random.key(seed)
        ks = jax.random.split(key, 4)
        scale = 1.0 / np.sqrt(D)
        return {'hidden_states': jax.random.normal(ks[0], (B, S, D), jnp.float32), 'Wq': jax.random.normal(ks[1], (D, D), jnp.float32) * scale, 'bq': jnp.zeros((D,), jnp.float32), 'Wk': jax.random.normal(ks[2], (D, D), jnp.float32) * scale, 'bk': jnp.zeros((D,), jnp.float32), 'Wv': jax.random.normal(ks[3], (D, D), jnp.float32) * scale, 'bv': jnp.zeros((D,), jnp.float32)}
    _L0_attn_in = _L0_attn_setup()

    def _L0_ffn_setup():
        import jax, jax.numpy as jnp
        import numpy as np
        import math
        GOLDEN_CENTER = 1.0 / math.e
        GOLDEN_LOWER = 0.5 - math.log(4.0 / 3.0)
        GOLDEN_UPPER = 0.5
        B, T, D = (4, 256, 128)
        E = 8
        I = 512 // (E // 2)

        def _routing_weights(x, Wr, temperature):
            inh = jax.nn.sigmoid(x @ Wr / temperature)
            in_zone = (inh >= GOLDEN_LOWER) & (inh <= GOLDEN_UPPER)
            dist = jnp.abs(inh - GOLDEN_CENTER)
            w = jnp.exp(-dist / 0.1) * in_zone.astype(x.dtype)
            wsum = w.sum(axis=-1, keepdims=True)
            no_expert = wsum < 1e-08
            fb = jnp.exp(-dist / 0.3)
            _, top2 = jax.lax.top_k(fb, 2)
            fb_mask = jax.nn.one_hot(top2, E, dtype=x.dtype).sum(axis=-2)
            fb_w = fb * fb_mask
            fb_w = fb_w / jnp.clip(fb_w.sum(axis=-1, keepdims=True), 1e-08)
            w = jnp.where(no_expert, fb_w, w)
            wsum = w.sum(axis=-1, keepdims=True)
            return w / jnp.clip(wsum, 1e-08)
        key = jax.random.key(seed)
        k = jax.random.split(key, 6)
        s_d = 1.0 / math.sqrt(D)
        s_i = 1.0 / math.sqrt(I)
        return {'x': jax.random.normal(k[0], (B, T, D), jnp.float32), 'Wg': jax.random.normal(k[1], (E, D, I), jnp.float32) * s_d, 'Wu': jax.random.normal(k[2], (E, D, I), jnp.float32) * s_d, 'Wd': jax.random.normal(k[3], (E, I, D), jnp.float32) * s_i, 'Wr': jax.random.normal(k[4], (D, E), jnp.float32) * s_d, 'temperature': jnp.ones((1,), jnp.float32)}
    _L0_ffn_in = _L0_ffn_setup()
    _L0_c = _w((lambda *s: np.random.randn(*s).astype(np.float32) * 0.05)(1, 128))
    _L0_wmod = _w((lambda *s: np.random.randn(*s).astype(np.float32) * 0.05)(128, 6 * 128) * 128 ** (-0.5))
    _d = {'L0_attn_hidden_states': _L0_attn_in['hidden_states'], 'L0_attn_Wq': _L0_attn_in['Wq'], 'L0_attn_bq': _L0_attn_in['bq'], 'L0_attn_Wk': _L0_attn_in['Wk'], 'L0_attn_bk': _L0_attn_in['bk'], 'L0_attn_Wv': _L0_attn_in['Wv'], 'L0_attn_bv': _L0_attn_in['bv'], 'L0_ffn_Wg': _L0_ffn_in['Wg'], 'L0_ffn_Wu': _L0_ffn_in['Wu'], 'L0_ffn_Wd': _L0_ffn_in['Wd'], 'L0_ffn_Wr': _L0_ffn_in['Wr'], 'L0_ffn_temperature': _L0_ffn_in['temperature'], 'L0_c': _L0_c, 'L0_wmod': _L0_wmod}
    _x0 = _d['L0_attn_hidden_states']
    _d['L0_attn_hidden_states'] = jax.random.normal(jax.random.fold_in(jax.random.key(seed), 1), (1, 2048, 128), dtype=_x0.dtype)
    del _x0
    return _d

def reference(L0_attn_hidden_states, L0_attn_Wq, L0_attn_bq, L0_attn_Wk, L0_attn_bk, L0_attn_Wv, L0_attn_bv, L0_ffn_Wg, L0_ffn_Wu, L0_ffn_Wd, L0_ffn_Wr, L0_ffn_temperature, L0_c, L0_wmod):

    def _L0_attn_ref(hidden_states, Wq, bq, Wk, bk, Wv, bv):
        import jax, jax.numpy as jnp
        import numpy as np
        B, S, D = (2, 256, 128)
        H = 16
        HD = D // H

        def _rope_tables(seq_len, head_dim, dtype):
            pos = jnp.arange(seq_len, dtype=dtype)
            inv = jnp.power(10000.0, -2.0 * jnp.arange(head_dim // 2, dtype=dtype) / head_dim)
            ang = pos[:, None] * inv[None, :]
            cos_pos = jnp.repeat(jnp.cos(ang), 2, axis=-1)
            sin_pos = jnp.repeat(jnp.sin(ang), 2, axis=-1)
            return (cos_pos, sin_pos)

        def _rotate_half_interleaved(x):
            x2 = jnp.stack([-x[..., 1::2], x[..., 0::2]], axis=-1)
            return x2.reshape(x.shape)
        b, s, d = hidden_states.shape
        q = hidden_states @ Wq + bq
        k = hidden_states @ Wk + bk
        v = hidden_states @ Wv + bv
        q = q.reshape(b, s, H, HD).transpose(0, 2, 1, 3)
        k = k.reshape(b, s, H, HD).transpose(0, 2, 1, 3)
        v = v.reshape(b, s, H, HD).transpose(0, 2, 1, 3)
        cos_pos, sin_pos = _rope_tables(s, HD, hidden_states.dtype)
        q = q * cos_pos + _rotate_half_interleaved(q) * sin_pos
        k = k * cos_pos + _rotate_half_interleaved(k) * sin_pos
        scores = jnp.einsum('bhqd,bhkd->bhqk', q, k) / jnp.sqrt(jnp.asarray(HD, hidden_states.dtype))
        probs = jax.nn.softmax(scores, axis=-1)
        ctx = jnp.einsum('bhqk,bhkd->bhqd', probs, v)
        ctx = ctx.transpose(0, 2, 1, 3).reshape(b, s, d)
        return ctx

    def _L0_ffn_ref(x, Wg, Wu, Wd, Wr, temperature):
        import jax, jax.numpy as jnp
        import numpy as np
        import math
        GOLDEN_CENTER = 1.0 / math.e
        GOLDEN_LOWER = 0.5 - math.log(4.0 / 3.0)
        GOLDEN_UPPER = 0.5
        B, T, D = (4, 256, 128)
        E = 8
        I = 512 // (E // 2)

        def _routing_weights(x, Wr, temperature):
            inh = jax.nn.sigmoid(x @ Wr / temperature)
            in_zone = (inh >= GOLDEN_LOWER) & (inh <= GOLDEN_UPPER)
            dist = jnp.abs(inh - GOLDEN_CENTER)
            w = jnp.exp(-dist / 0.1) * in_zone.astype(x.dtype)
            wsum = w.sum(axis=-1, keepdims=True)
            no_expert = wsum < 1e-08
            fb = jnp.exp(-dist / 0.3)
            _, top2 = jax.lax.top_k(fb, 2)
            fb_mask = jax.nn.one_hot(top2, E, dtype=x.dtype).sum(axis=-2)
            fb_w = fb * fb_mask
            fb_w = fb_w / jnp.clip(fb_w.sum(axis=-1, keepdims=True), 1e-08)
            w = jnp.where(no_expert, fb_w, w)
            wsum = w.sum(axis=-1, keepdims=True)
            return w / jnp.clip(wsum, 1e-08)
        weights = _routing_weights(x, Wr, temperature)
        gate = jnp.einsum('btd,edi->beti', x, Wg)
        up = jnp.einsum('btd,edi->beti', x, Wu)
        h = jax.nn.silu(gate) * up
        e_out = jnp.einsum('beti,eid->betd', h, Wd)
        out = jnp.einsum('bte,betd->btd', weights, e_out)
        return out
    x = L0_attn_hidden_states
    mod = (_silu(L0_c) @ L0_wmod).reshape(L0_c.shape[0], 6, 1, -1)
    sa, ca, ga, sb, cb, gb = (mod[:, 0], mod[:, 1], mod[:, 2], mod[:, 3], mod[:, 4], mod[:, 5])
    ga = (2 * (ga >= 0) - 1) * jnp.maximum(jnp.abs(ga), 0.25)
    gb = (2 * (gb >= 0) - 1) * jnp.maximum(jnp.abs(gb), 0.25)
    h = _layernorm(x, axis=-1) * (1 + ca) + sa
    x = x + ga * _L0_attn_ref(h, L0_attn_Wq, L0_attn_bq, L0_attn_Wk, L0_attn_bk, L0_attn_Wv, L0_attn_bv)
    h = _layernorm(x, axis=-1) * (1 + cb) + sb
    x = x + gb * _L0_ffn_ref(h, L0_ffn_Wg, L0_ffn_Wu, L0_ffn_Wd, L0_ffn_Wr, L0_ffn_temperature)
    return x

_drawn_inputs = setup_inputs


def setup_inputs(seed=0):
    import zlib

    import numpy as np

    out = dict(_drawn_inputs(seed))
    spreads = {'L0_attn_bq': (0.0, 0.8), 'L0_attn_bk': (0.0, 0.8), 'L0_attn_bv': (0.0, 0.296)}
    factors = {'L0_attn_Wq': 4.054, 'L0_attn_Wk': 3.741, 'L0_attn_Wv': 3.631}
    for name, (base, spread) in spreads.items():
        noise = np.random.default_rng([zlib.crc32(name.encode()), seed]).standard_normal(out[name].shape)
        drawn = base * np.exp(spread * noise) if base else spread * noise
        out[name] = jnp.asarray(drawn.astype(out[name].dtype))
    for name, factor in factors.items():
        out[name] = (out[name] * factor).astype(out[name].dtype)
    return out
```

```python
from contextlib import ExitStack

import numpy as np

import concourse.bass as bass
from concourse import mybir

F32 = mybir.dt.float32
BF16 = mybir.dt.bfloat16
ACT = mybir.ActivationFunctionType
ALU = mybir.AluOpType
AX_X = mybir.AxisListType.X

P = 128
D = 128
S = 2048
H = 16
HD = D // H
NT = S // P
BANK = 512
NB = S // BANK
TPB = BANK // P
E = 8
EI = 128
EPS = 1e-5
SCALE = 1.0 / float(np.sqrt(np.float32(HD)))

SPLITS = 3
BLOCK = HD * SPLITS
ROWS = BLOCK * SPLITS
SHIFT_ROW = 96
SCORE_ROWS = SHIFT_ROW
LEAD = 4
PRO = NT + LEAD
PAIR = 2 * NT
EB, MB, ACC, AUX = 0, 3, 6, 7
RING = 3
PSLOTS = 4
MOPS = 4


def previous(k):
    return k - RING if k >= RING else {0: -2, 1: -1, 2: -3}[k]


def adaln_block(nc, x, wq, bq, wk, bk, wv, bv, wg, wu, wd, wr, temp, c, wmod, cos_t, sin_t, ident, tri, out):
    with ExitStack() as ctx:
        def sb(name, shape, dt=F32):
            return ctx.enter_context(nc.sbuf_tensor(name, shape, dt))

        def sem(name):
            return ctx.enter_context(nc.semaphore(name))

        split_dram = nc.dram_tensor("qk_split_scratch", [2, D, SPLITS, S], BF16).ap()
        ps = ctx.enter_context(nc.psum_tensor("ps", [P, 8, BANK], F32))

        x_sb = sb("x_sb", [P, NT, D])
        w_sb = sb("w_sb", [P, 5, D])
        b_row = sb("b_row", [1, 5, D])
        b_col = sb("b_col", [P, 4])
        id_f = sb("id_f", [P, P])
        id_b = sb("id_b", [P, P], BF16)
        ones_row = sb("ones_row", [1, P])
        wmod_sb = sb("wmod_sb", [P, 6 * D])
        cs = sb("cs", [P, 8])
        silu_b = sb("silu_b", [P, P])
        mod = sb("mod", [P, 6])
        gate_raw = sb("gate_raw", [P, 2, D])
        gate_sgn = sb("gate_sgn", [P, 2, D])
        gate_abs = sb("gate_abs", [P, 2, D])
        gate = sb("gate", [P, 2, D])
        wg_sb = sb("wg_sb", [P, E, EI])
        wu_sb = sb("wu_sb", [P, E, EI])
        wd_sb = sb("wd_sb", [P, E, D])
        wr_sb = sb("wr_sb", [P, E])
        temp_sb = sb("temp_sb", [P, 2])
        tri_sb = sb("tri_sb", [P, E, E])

        stats = sb("stats", [P, NT, 6])
        mv = sb("mv", [P, NT, 2])
        var_e = sb("var_e", [P, NT])
        mhalf = sb("mhalf", [P, NT])
        rstd = sb("rstd", [P, NT])
        z_sb = sb("z_sb", [P, NT, D])
        hT = sb("hT", [P, S])

        v_sb = sb("v_sb", [P, NT, D])
        parts = sb("parts", [P, 2, SPLITS, S], BF16)
        m_q = sb("m_q", [P, 2, S], BF16)
        m_k = sb("m_k", [P, 2, S], BF16)
        e_q = sb("e_q", [P, 2, S], BF16)
        e_k = sb("e_k", [P, 2, S], BF16)
        probs = sb("probs", [P, PSLOTS, S])
        v_head = sb("v_head", [P, 2, NT, 32])
        m_part = sb("m_part", [P, 2, NT, NB])
        m_neg = sb("m_neg", [P, NT])
        m_rest = sb("m_rest", [P, NT])
        m_split = sb("m_split", [P, P], BF16)
        mT = sb("mT", [SPLITS * NT, P], BF16)
        cx = sb("cx", [P, BANK])
        rsum = sb("rsum", [P, TPB, NB])
        ctx_sb = sb("ctx_sb", [P, NT, D])

        cos_sb, sin_sb = probs[:, 0, :], probs[:, 1, :]
        qk_f = probs[:, 2, :]
        qk_t = probs[:, 3, :]

        rt = sb("rt", [P, 14, NT * E])
        cmp = sb("cmp", [P, 2, NT * E * E])
        rs2 = sb("rs2", [P, 8, NT])
        sg = [probs[:, 0, i * BANK:(i + 1) * BANK] for i in range(2)]
        hh = [probs[:, 1, i * BANK:(i + 1) * BANK] for i in range(2)]
        y_sb = probs[:, 2, :].rearrange("p (t d) -> p t d", d=D)
        o_sb = probs[:, 3, :].rearrange("p (t d) -> p t d", d=D)

        x_in = sem("x_in")
        w_in = sem("w_in")
        b_in = sem("b_in")
        c_in = sem("c_in")
        mod_in = sem("mod_in")
        t_in = sem("t_in")
        f_in = sem("f_in")
        id_in = sem("id_in")
        ones = sem("ones")
        dch = sem("dch")
        ach = sem("ach")
        pch = sem("pch")
        stat_ok = sem("stat_ok")
        rstd_ok = sem("rstd_ok")
        z_ok = sem("z_ok")
        zT = sem("zT")
        hT_ok = sem("hT_ok")
        w_rot = sem("w_rot")
        col_mm = sem("col_mm")
        col_ok = sem("col_ok")
        mod_mm = sem("mod_mm")
        mod_ok = sem("mod_ok")
        gate_mm = sem("gate_mm")
        silu_ok = sem("silu_ok")
        e1 = sem("e1")
        proj = sem("proj")
        rope = sem("rope")
        part1 = sem("part1")
        rest1 = sem("rest1")
        part2 = sem("part2")
        part3 = sem("part3")
        split_out = sem("split_out")
        vproj = sem("vproj")
        v_ok = sem("v_ok")
        pad_ok = sem("pad_ok")
        s_full = sem("s_full")
        p_done = sem("p_done")
        m_full = sem("m_full")
        m_done = sem("m_done")
        pv_done = sem("pv_done")
        m_ready = sem("m_ready")
        mT_mm = sem("mT_mm")
        mT_ok = sem("mT_ok")
        cx_ok = sem("cx_ok")
        cxT = sem("cxT")
        ctx_ok = sem("ctx_ok")
        vh_ok = sem("vh_ok")
        x1_ok = sem("x1_ok")
        stat2_ok = sem("stat2_ok")
        rstd2_ok = sem("rstd2_ok")
        z2_ok = sem("z2_ok")
        zT2 = sem("zT2")
        hT2_ok = sem("hT2_ok")
        log_mm = sem("log_mm")
        sig_in = sem("sig_in")
        sig_e = sem("sig_e")
        wexp_in = sem("wexp_in")
        wexp = sem("wexp")
        route_ok = sem("route_ok")
        gu_mm = sem("gu_mm")
        silu_done = sem("silu_done")
        h_ok = sem("h_ok")
        down_mm = sem("down_mm")
        comb_ok = sem("comb_ok")
        y_ok = sem("y_ok")
        out_ok = sem("out_ok")
        setm = [sem("setm0"), sem("setm1")]
        sete = [sem("sete0"), sem("sete1")]
        shift = [sem("shift0"), sem("shift1")]

        block = ctx.enter_context(nc.Block())

        def operand_rows(sp, dst_q, dst_k, b, h, done):
            h8 = h * HD
            qs = split_dram[0, bass.ds(h8, HD)] if not isinstance(h, int) else split_dram[0, h8:h8 + HD]
            ks = split_dram[1, bass.ds(h8, HD)] if not isinstance(h, int) else split_dram[1, h8:h8 + HD]
            for i in range(SPLITS):
                rows = slice(i * BLOCK, (i + 1) * BLOCK)
                sp.dma_start(dst_q[rows, b, :],
                             qs[:, i:i + 1, :].broadcast_to([HD, SPLITS, S])).then_inc(done, 16)
                sp.dma_start(dst_k[rows, b, :], ks.rearrange("d j n -> (d j) n")).then_inc(done, 16)

        SET = 2 * SPLITS * 16

        @block.sync
        def _(sp):
            for i in range(4):
                t = slice(i * TPB, (i + 1) * TPB)
                sp.dma_start(x_sb[:, t, :], x[0].rearrange("(t p) d -> p t d", p=P)[:, t, :]).then_inc(x_in, 16)
            sp.dma_start(cos_sb, cos_t).then_inc(t_in, 16)
            sp.dma_start(sin_sb, sin_t).then_inc(t_in, 16)
            sp.dma_start(wg_sb[:], wg.rearrange("e d i -> d e i")).then_inc(f_in, 16)
            sp.dma_start(wu_sb[:], wu.rearrange("e d i -> d e i")).then_inc(f_in, 16)
            sp.dma_start(wd_sb[:], wd.rearrange("e i d -> i e d")).then_inc(f_in, 16)
            sp.dma_start(wr_sb[:], wr).then_inc(f_in, 16)
            sp.dma_start(temp_sb[:, 0:1], temp.rearrange("(a b) -> a b", a=1).broadcast_to([P, 1])).then_inc(f_in, 16)
            sp.dma_start(tri_sb[:], tri).then_inc(f_in, 16)
            for qk in range(2):
                sp.wait_ge(part3, NB * (qk + 1))
                sp.wait_ge(part2, NB * (qk + 1))
                sp.wait_ge(part1, NB * (qk + 1))
                sp.dma_start(split_dram[qk], parts[:, qk]).then_inc(split_out, 16)
            sp.wait_ge(split_out, 32)
            sp.wait_ge(pad_ok, 9)
            operand_rows(sp, m_q, m_k, 0, 0, setm[0])
            operand_rows(sp, m_q, m_k, 1, 1, setm[1])
            operand_rows(sp, e_q, e_k, 0, 0, sete[0])

            def shift_rows(h, b):
                sp.wait_ge(mT_ok, h + 1)
                sp.dma_start(e_q[SHIFT_ROW:SHIFT_ROW + SPLITS, b, :].rearrange("i (t p) -> i t p", p=P),
                             mT[:]).then_inc(shift[b], 16)

            shift_rows(0, 0)

            def pair(p, first=False, last=False):
                if not last:
                    sp.wait_ge(m_done, (2 * p + 1) * NT * NB)
                    operand_rows(sp, m_q, m_k, 0, 2 * p + 2, setm[0])
                if not first:
                    sp.wait_ge(pv_done, 2 * p * NT)
                operand_rows(sp, e_q, e_k, 1, 2 * p + 1, sete[1])
                shift_rows(2 * p + 1, 1)
                if not last:
                    sp.wait_ge(m_done, (2 * p + 2) * NT * NB)
                    operand_rows(sp, m_q, m_k, 1, 2 * p + 3, setm[1])
                    sp.wait_ge(pv_done, (2 * p + 1) * NT)
                    operand_rows(sp, e_q, e_k, 0, 2 * p + 2, sete[0])
                    shift_rows(2 * p + 2, 0)

            pair(0, first=True)
            with sp.Fori(1, H // 2 - 1) as p:
                pair(p)
            pair(H // 2 - 1, last=True)
            sp.wait_ge(out_ok, NB)
            for i in range(NB):
                t = slice(i * TPB, (i + 1) * TPB)
                sp.dma_start(out[0].rearrange("(t p) d -> p t d", p=P)[:, t, :], o_sb[:, t, :]).then_inc(y_ok, 16)
            sp.wait_ge(y_ok, 16 * NB)

        @block.gpsimd
        def _(pool):
            nc.gpsimd.memset(mhalf[:], -0.5).then_inc(pad_ok, 1)
            pool.wait_ge(pad_ok, 1)
            pool.wait_ge(stat_ok, 1)
            nc.gpsimd.tensor_tensor(rstd[:], var_e[:], mhalf[:], ALU.pow).then_inc(rstd_ok, 1)
            pool.wait_ge(rstd_ok, 1)
            pads = [(m_q[64:96, :, :].bitcast(F32), 0.0), (m_k[64:96, :, :].bitcast(F32), 0.0),
                    (e_q[64:128, :, :].bitcast(F32), 0.0), (e_k[64:128, :, :].bitcast(F32), 0.0),
                    (e_k[SHIFT_ROW:SHIFT_ROW + SPLITS, :, :], 1.0),
                    (m_split[:], 0.0), (v_head[:], 0.0), (v_head[:, :, :, HD:HD + 1], 1.0)]
            for n, (buf, value) in enumerate(pads):
                nc.gpsimd.memset(buf, value).then_inc(pad_ok, 1)
                pool.wait_ge(pad_ok, n + 2)
            pool.wait_ge(v_ok, NB)

            def pair(p, first=False, last=False):
                for b in range(2):
                    h = 2 * p + b
                    if not first:
                        pool.wait_ge(pv_done, (h - 1) * NT)
                    src = v_sb[:, :, h * HD:(h + 1) * HD] if isinstance(h, int) else v_sb[:, :, bass.ds(h * HD, HD)]
                    nc.gpsimd.tensor_copy(v_head[:, b, :, 0:HD], src).then_inc(vh_ok, 1)

            pair(0, first=True)
            with pool.Fori(1, H // 2 - 1) as p:
                pair(p)
            pair(H // 2 - 1, last=True)
            pool.wait_ge(stat2_ok, 1)
            nc.gpsimd.tensor_tensor(rstd[:], var_e[:], mhalf[:], ALU.pow).then_inc(rstd2_ok, 1)

        @block.scalar
        def _(act):
            act.dma_start(cs[:, 0:1], c.rearrange("a d -> d a")).then_inc(c_in, 16)
            act.dma_start(wmod_sb[:], wmod).then_inc(mod_in, 16)
            act.dma_start(id_f[:], ident).then_inc(id_in, 16)
            for i, w in ((0, wq), (2, wk), (4, wv)):
                act.dma_start(w_sb[:, i, :], w).then_inc(w_in, 16)
            for i, b in ((0, bq), (2, bk), (4, bv)):
                act.dma_start(b_row[0:1, i, :], b.rearrange("(a d) -> a d", a=1)).then_inc(b_in, 16)
            act.wait_ge(c_in, 16)
            nc.scalar.activation(cs[:, 1:2], cs[:, 0:1], ACT.Exp, scale=-1.0).then_inc(e1, 1)
            act.wait_ge(id_in, 16)
            nc.scalar.copy(id_b[:], id_f[:]).then_inc(ach, 1)
            act.wait_ge(mod_ok, 1)
            for n in range(NB):
                act.wait_ge(zT, n + 1)
                nc.scalar.activation(hT[:, n * BANK:(n + 1) * BANK], ps[:, n, :], ACT.Identity,
                                     bias=mod[:, 0:1], scale=mod[:, 1:2]).then_inc(hT_ok, 1)
            for n in range(NB):
                act.wait_ge(vproj, n + 1)
                nc.scalar.copy(v_sb[:, n * TPB:(n + 1) * TPB, :],
                               ps[:, 4 + n, :].rearrange("p (t d) -> p t d", d=D)).then_inc(v_ok, 1)
            for qk in range(2):
                for n in range(NB):
                    col = slice(n * BANK, (n + 1) * BANK)
                    act.wait_ge(rope, qk * NB + n + 1)
                    nc.scalar.copy(parts[:, qk, 0, col], qk_f[:, col]).then_inc(part1, 1)
                    act.wait_ge(rest1, qk * NB + n + 1)
                    nc.scalar.copy(parts[:, qk, 1, col], qk_t[:, col]).then_inc(part2, 1)

            def shift_copy(h):
                act.wait_ge(mT_mm, h + 1)
                nc.scalar.copy(mT[:], ps[0:SPLITS * NT, AUX, 0:P // 2].bitcast(BF16)).then_inc(mT_ok, 1)

            act.wait_ge(part3, 2 * NB)
            shift_copy(0)

            def pair(p, first=False, last=False):
                for k in range(PAIR):
                    step = p * PAIR + k
                    if k in (PAIR // 2 - 2, PAIR - 2) and not (last and k > NT):
                        b = 1 if k < NT else 0
                        h = 2 * p + (1 if k < NT else 2)
                        act.wait_ge(mT_mm, h + 1)
                        act.wait_ge(shift[1 - b], 16 * (p + 1))
                        nc.scalar.copy(mT[:], ps[0:SPLITS * NT, AUX, 0:P // 2].bitcast(BF16)).then_inc(mT_ok, 1)
                    if not first or k >= PSLOTS:
                        act.wait_ge(pv_done, step - PSLOTS + 1)
                    for j in range(NB):
                        q = 4 * k + j
                        act.wait_ge(s_full, p * PAIR * NB + q + 1)
                        nc.scalar.activation(probs[:, k % PSLOTS, j * BANK:(j + 1) * BANK],
                                             ps[:, EB + q % RING, :], ACT.Exp, scale=SCALE).then_inc(p_done, 1)
                    if k % NT == 0 and not (first and k == 0):
                        h = 2 * p + k // NT - 1
                        act.wait_ge(pv_done, (h + 1) * NT)
                        if not first:
                            act.wait_ge(cxT, h)
                        nc.scalar.copy(cx[:], ps[:, ACC, :]).then_inc(cx_ok, 1)

            pair(0, first=True)
            with act.Fori(1, H // 2 - 1) as p:
                pair(p)
            pair(H // 2 - 1, last=True)
            act.wait_ge(pv_done, H * NT)
            act.wait_ge(cxT, H - 1)
            nc.scalar.copy(cx[:], ps[:, ACC, :]).then_inc(cx_ok, 1)

            for n in range(NB):
                act.wait_ge(zT2, n + 1)
                nc.scalar.activation(hT[:, n * BANK:(n + 1) * BANK], ps[:, n, :], ACT.Identity,
                                     bias=mod[:, 3:4], scale=mod[:, 4:5]).then_inc(hT2_ok, 1)
            act.wait_ge(sig_in, 1)
            nc.scalar.activation(rt[:, 1], rt[:, 0], ACT.Exp).then_inc(sig_e, 1)
            act.wait_ge(wexp_in, 1)
            nc.scalar.activation(rt[:, 5], rt[:, 4], ACT.Exp, scale=-1.0 / 0.1).then_inc(wexp, 1)
            nc.scalar.activation(rt[:, 6], rt[:, 4], ACT.Exp, scale=-1.0 / 0.3).then_inc(wexp, 1)
            for n in range(NB * E):
                act.wait_ge(gu_mm, n + 1)
                if n >= 2:
                    act.wait_ge(h_ok, n - 1)
                nc.scalar.activation(sg[n % 2], ps[:, 2 * (n % 2), :], ACT.Silu).then_inc(silu_done, 1)

        @block.vector
        def _(dve):
            count = [0]

            def link(ins):
                count[0] += 1
                ins.then_inc(dch, 1)
                dve.wait_ge(dch, count[0])

            nc.vector.memset(ones_row[:], 1.0).then_inc(ones, 1)
            for n in range(NB):
                dve.wait_ge(x_in, 16 * NB)
                for t in range(n * TPB, (n + 1) * TPB):
                    last = nc.vector.bn_stats(stats[:, t, :], x_sb[:, t, :])
            link(last)
            for t in range(NT):
                last = nc.vector.bn_aggr(mv[:, t, :], stats[:, t, :])
            link(last)
            nc.vector.tensor_scalar(var_e[:], mv[:, :, 1], EPS, None, ALU.add).then_inc(stat_ok, 1)
            dve.wait_ge(e1, 1)
            link(nc.vector.tensor_scalar(cs[:, 2:3], cs[:, 1:2], 1.0, None, ALU.add))
            link(nc.vector.reciprocal(cs[:, 3:4], cs[:, 2:3]))
            link(nc.vector.tensor_tensor(cs[:, 4:5], cs[:, 0:1], cs[:, 3:4], ALU.mult))
            nc.vector.tensor_copy(silu_b[:], cs[:, 4:5].broadcast_to([P, P])).then_inc(silu_ok, 1)
            dve.wait_ge(w_in, 48)
            dve.wait_ge(b_in, 48)
            for i in (0, 2):
                for src, dst in ((w_sb[:, i, :], w_sb[:, i + 1, :]), (b_row[0:1, i, :], b_row[0:1, i + 1, :])):
                    sv = src.rearrange("p (m e) -> p m e", e=2)
                    dv = dst.rearrange("p (m e) -> p m e", e=2)
                    nc.vector.tensor_scalar(dv[:, :, 0], sv[:, :, 1], -1.0, None, ALU.mult).then_inc(w_rot, 1)
                    nc.vector.tensor_copy(dv[:, :, 1], sv[:, :, 0]).then_inc(w_rot, 1)
            dve.wait_ge(rstd_ok, 1)
            for t in range(NT):
                nc.vector.tensor_scalar(z_sb[:, t, :], x_sb[:, t, :], mv[:, t, 0:1], rstd[:, t:t + 1],
                                        ALU.subtract, ALU.mult).then_inc(z_ok, 1)
            dve.wait_ge(mod_mm, 1)
            link(nc.vector.tensor_copy(mod[:], ps[:, 7, 0:6]))
            nc.vector.tensor_scalar(mod[:].rearrange("p (a b) -> p a b", b=3)[:, :, 1],
                                    mod[:].rearrange("p (a b) -> p a b", b=3)[:, :, 1], 1.0, None,
                                    ALU.add).then_inc(mod_ok, 1)
            dve.wait_ge(gate_mm, 1)
            link(nc.vector.tensor_copy(gate_raw[:], ps[:, 6, 0:2 * D].rearrange("p (a d) -> p a d", a=2)))
            dve.wait_ge(col_mm, 1)
            nc.vector.tensor_copy(b_col[:], ps[:, 5, 0:4]).then_inc(col_ok, 1)
            link(nc.vector.tensor_scalar(gate_abs[:], gate_raw[:], -1.0, None, ALU.mult))
            link(nc.vector.tensor_tensor(gate_abs[:], gate_abs[:], gate_raw[:], ALU.max))
            link(nc.vector.tensor_scalar(gate_abs[:], gate_abs[:], 0.25, None, ALU.max))
            link(nc.vector.tensor_scalar(gate_sgn[:], gate_raw[:], 0.0, 2.0, ALU.is_ge, ALU.mult))
            link(nc.vector.tensor_scalar(gate_sgn[:], gate_sgn[:], -1.0, None, ALU.add))
            link(nc.vector.tensor_tensor(gate[:], gate_sgn[:], gate_abs[:], ALU.mult))
            dve.wait_ge(col_ok, 1)
            dve.wait_ge(t_in, 32)
            for qk in range(2):
                for n in range(NB):
                    i = qk * NB + n
                    col = slice(n * BANK, (n + 1) * BANK)
                    dve.wait_ge(proj, i + 1)
                    bank = 2 * (i % 2)
                    if i >= NB:
                        dve.wait_ge(part2, i - NB + 1)
                    link(nc.vector.scalar_tensor_tensor(qk_f[:, col], ps[:, bank, :], b_col[:, 2 * qk:2 * qk + 1],
                                                        cos_sb[:, col], ALU.add, ALU.mult))
                    link(nc.vector.scalar_tensor_tensor(qk_t[:, col], ps[:, bank + 1, :], b_col[:, 2 * qk + 1:2 * qk + 2],
                                                        sin_sb[:, col], ALU.add, ALU.mult))
                    nc.vector.tensor_tensor(qk_f[:, col], qk_f[:, col], qk_t[:, col], ALU.add).then_inc(rope, 1)
                    dve.wait_ge(part1, i + 1)
                    nc.vector.tensor_tensor(qk_t[:, col], qk_f[:, col], parts[:, qk, 0, col],
                                            ALU.subtract).then_inc(rest1, 1)
                    dve.wait_ge(part2, i + 1)
                    nc.vector.tensor_tensor(parts[:, qk, 2, col], qk_t[:, col], parts[:, qk, 1, col],
                                            ALU.subtract).then_inc(part3, 1)

            base = count[0]

            def chain(ins, h, n):
                ins.then_inc(dch, 1)
                dve.wait_ge(dch, base + h * MOPS + n + 1)

            def max_step(m, b, k, before=0):
                for j in range(NB):
                    dve.wait_ge(m_full, m * NB + j + 1)
                    nc.vector.tensor_reduce(m_part[:, b, k % NT, j:j + 1], ps[:, MB + (NB * before + j) % RING, :],
                                            AX_X, ALU.max).then_inc(m_done, 1)

            def max_head(h, b, first=False):
                dve.wait_ge(m_done, (h + 1) * NT * NB)
                if not first:
                    dve.wait_ge(mT_mm, h)
                chain(nc.vector.tensor_reduce(m_neg[:], m_part[:, b], AX_X, ALU.max, negate=True), h, 0)
                chain(nc.vector.tensor_copy(m_split[:, 0:NT], m_neg[:]), h, 1)
                chain(nc.vector.tensor_tensor(m_rest[:], m_neg[:], m_split[:, 0:NT], ALU.subtract), h, 2)
                chain(nc.vector.tensor_copy(m_split[:, NT:2 * NT], m_rest[:]), h, 3)
                nc.vector.tensor_tensor(m_split[:, 2 * NT:3 * NT], m_rest[:], m_split[:, NT:2 * NT],
                                        ALU.subtract).then_inc(m_ready, 1)

            def normalise(h):
                dve.wait_ge(cxT, h + 1)
                aux = ps[:, AUX, :].rearrange("p (c j r) -> p c j r", c=TPB, r=32)
                nc.vector.reciprocal(rsum[:], aux[:, :, :, HD]).then_inc(pch, 1)
                dve.wait_ge(pch, h + 1)
                dst = ctx_sb[:, :, h * HD:(h + 1) * HD] if isinstance(h, int) else ctx_sb[:, :, bass.ds(h * HD, HD)]
                nc.vector.tensor_tensor(dst.rearrange("p (j c) d -> p c j d", c=TPB), aux[:, :, :, 0:HD],
                                        rsum[:].unsqueeze(3).broadcast_to([P, TPB, NB, HD]),
                                        ALU.mult).then_inc(ctx_ok, 1)

            dve.wait_ge(pad_ok, 9)
            for m in range(PRO):
                max_step(m, m // NT, m, m)
                if m == NT - 1:
                    max_head(0, 0, first=True)

            def pair(p, first=False, last=False):
                for k in range(PAIR):
                    m = k + PRO
                    if not last or m < PAIR:
                        max_step(p * PAIR + m, (m // NT) % 2, m, k)
                        if m % NT == NT - 1:
                            max_head(2 * p + m // NT, (m // NT) % 2)
                    if k % NT == 2 and not (first and k == 2):
                        normalise(2 * p + k // NT - 1)

            pair(0, first=True)
            with dve.Fori(1, H // 2 - 1) as p:
                pair(p)
            pair(H // 2 - 1, last=True)
            normalise(H - 1)
            count[0] = base + H * MOPS

            dve.wait_ge(ctx_ok, H)
            link(nc.vector.tensor_tensor(ctx_sb[:], ctx_sb[:], gate[:, 0:1, :].broadcast_to([P, NT, D]), ALU.mult))
            link(nc.vector.tensor_tensor(x_sb[:], x_sb[:], ctx_sb[:], ALU.add))
            for t in range(NT):
                last = nc.vector.bn_stats(stats[:, t, :], x_sb[:, t, :])
            link(last)
            for t in range(NT):
                last = nc.vector.bn_aggr(mv[:, t, :], stats[:, t, :])
            link(last)
            nc.vector.tensor_scalar(var_e[:], mv[:, :, 1], EPS, None, ALU.add).then_inc(stat2_ok, 1)
            dve.wait_ge(f_in, 96)
            link(nc.vector.reciprocal(temp_sb[:, 1:2], temp_sb[:, 0:1]))
            dve.wait_ge(rstd2_ok, 1)
            for t in range(NT):
                nc.vector.tensor_scalar(z_sb[:, t, :], x_sb[:, t, :], mv[:, t, 0:1], rstd[:, t:t + 1],
                                        ALU.subtract, ALU.mult).then_inc(z2_ok, 1)

            def te(i):
                return rt[:, i].rearrange("p (t e) -> p t e", e=E)

            def wide(a):
                return a.unsqueeze(2).broadcast_to([P, NT, E])

            dve.wait_ge(log_mm, 1)
            nc.vector.tensor_scalar(rt[:, 0], ps[:, 7, 0:NT * E], temp_sb[:, 1:2], -1.0, ALU.mult,
                                    ALU.mult).then_inc(sig_in, 1)
            dve.wait_ge(sig_e, 1)
            link(nc.vector.tensor_scalar(rt[:, 2], rt[:, 1], 1.0, None, ALU.add))
            link(nc.vector.reciprocal(rt[:, 3], rt[:, 2]))
            lower = float(0.5 - np.log(4.0 / 3.0))
            center = float(1.0 / np.e)
            link(nc.vector.tensor_scalar(rt[:, 0], rt[:, 3], -center, None, ALU.add))
            link(nc.vector.tensor_scalar(rt[:, 1], rt[:, 0], -1.0, None, ALU.mult))
            nc.vector.tensor_tensor(rt[:, 4], rt[:, 0], rt[:, 1], ALU.max).then_inc(wexp_in, 1)
            link(nc.vector.tensor_scalar(rt[:, 7], rt[:, 3], lower, None, ALU.is_ge))
            link(nc.vector.tensor_scalar(rt[:, 8], rt[:, 3], 0.5, None, ALU.is_le))
            link(nc.vector.tensor_tensor(rt[:, 7], rt[:, 7], rt[:, 8], ALU.mult))
            dve.wait_ge(wexp, 2)
            link(nc.vector.tensor_tensor(rt[:, 9], rt[:, 5], rt[:, 7], ALU.mult))
            link(nc.vector.tensor_reduce(rs2[:, 0], te(9), AX_X, ALU.add))
            link(nc.vector.tensor_scalar(rs2[:, 1], rs2[:, 0], 1e-8, None, ALU.is_lt))
            link(nc.vector.tensor_scalar(rs2[:, 2], rs2[:, 1], -1.0, 1.0, ALU.mult, ALU.add))
            mine = te(6).unsqueeze(3).broadcast_to([P, NT, E, E])
            other = te(6).unsqueeze(2).broadcast_to([P, NT, E, E])
            cm = [cmp[:, i].rearrange("p (t a b) -> p t a b", a=E, b=E) for i in range(2)]
            link(nc.vector.tensor_tensor(cm[0], other, mine, ALU.is_gt))
            link(nc.vector.tensor_tensor(cm[1], other, mine, ALU.is_equal))
            link(nc.vector.tensor_tensor(cm[1], cm[1], tri_sb[:].unsqueeze(1).broadcast_to([P, NT, E, E]), ALU.mult))
            link(nc.vector.tensor_tensor(cmp[:, 0], cmp[:, 0], cmp[:, 1], ALU.add))
            link(nc.vector.tensor_reduce(rt[:, 10], cmp[:, 0].rearrange("p (t b) -> p t b", b=E), AX_X, ALU.add))
            link(nc.vector.tensor_scalar(rt[:, 11], rt[:, 10], 2.0, None, ALU.is_lt))
            link(nc.vector.tensor_tensor(rt[:, 11], rt[:, 11], rt[:, 6], ALU.mult))
            link(nc.vector.tensor_reduce(rs2[:, 3], te(11), AX_X, ALU.add))
            link(nc.vector.tensor_scalar(rs2[:, 3], rs2[:, 3], 1e-8, None, ALU.max))
            link(nc.vector.reciprocal(rs2[:, 4], rs2[:, 3]))
            link(nc.vector.tensor_tensor(te(11), te(11), wide(rs2[:, 4]), ALU.mult))
            link(nc.vector.tensor_tensor(te(11), te(11), wide(rs2[:, 1]), ALU.mult))
            link(nc.vector.tensor_tensor(te(9), te(9), wide(rs2[:, 2]), ALU.mult))
            link(nc.vector.tensor_tensor(rt[:, 9], rt[:, 9], rt[:, 11], ALU.add))
            link(nc.vector.tensor_reduce(rs2[:, 5], te(9), AX_X, ALU.add))
            link(nc.vector.tensor_scalar(rs2[:, 5], rs2[:, 5], 1e-8, None, ALU.max))
            link(nc.vector.reciprocal(rs2[:, 6], rs2[:, 5]))
            link(nc.vector.tensor_tensor(te(12), te(9), wide(rs2[:, 6]), ALU.mult))

            def combine(n):
                dve.wait_ge(down_mm, n + 1)
                if n >= 1:
                    dve.wait_ge(comb_ok, TPB * n)
                e, tb = n % E, n // E
                for c in range(TPB):
                    t = tb * TPB + c
                    src = ps[:, 4 + n % 2, c * D:(c + 1) * D]
                    wt = te(12)[:, t, e:e + 1]
                    if e == 0:
                        last = nc.vector.tensor_scalar(y_sb[:, t, :], src, wt, None, ALU.mult)
                    else:
                        last = nc.vector.scalar_tensor_tensor(y_sb[:, t, :], src, wt, y_sb[:, t, :], ALU.mult, ALU.add)
                    last.then_inc(comb_ok, 1)
                if e == E - 1:
                    dve.wait_ge(comb_ok, TPB * (n + 1))
                    t = slice(tb * TPB, (tb + 1) * TPB)
                    link(nc.vector.tensor_tensor(y_sb[:, t, :], y_sb[:, t, :],
                                                 gate[:, 1:2, :].broadcast_to([P, TPB, D]), ALU.mult))
                    nc.vector.tensor_tensor(o_sb[:, t, :], x_sb[:, t, :], y_sb[:, t, :], ALU.add).then_inc(out_ok, 1)

            for n in range(NB * E):
                dve.wait_ge(silu_done, n + 1)
                if n >= 2:
                    dve.wait_ge(down_mm, n - 1)
                nc.vector.tensor_tensor(hh[n % 2], sg[n % 2], ps[:, 2 * (n % 2) + 1, :], ALU.mult).then_inc(h_ok, 1)
                if n >= 1:
                    combine(n - 1)
            combine(NB * E - 1)

        @block.tensor
        def _(pe):
            mm = nc.tensor.matmul
            pe.wait_ge(id_in, 16)
            pe.wait_ge(silu_ok, 1)
            pe.wait_ge(mod_in, 16)
            for i in range(6):
                last = mm(ps[:, 7, i:i + 1], wmod_sb[:, i * D:(i + 1) * D], cs[:, 4:5], start=True, stop=True)
            last.then_inc(mod_mm, 1)
            for i, g in enumerate((2, 5)):
                last = mm(ps[:, 6, i * D:(i + 1) * D], silu_b[:], wmod_sb[:, g * D:(g + 1) * D], start=True, stop=True)
            last.then_inc(gate_mm, 1)
            pe.wait_ge(w_rot, 8)
            pe.wait_ge(ones, 1)
            for i in range(4):
                last = mm(ps[:, 5, i:i + 1], b_row[0:1, i, :], ones_row[0:1, 0:1], start=True, stop=True)
            last.then_inc(col_mm, 1)
            for n in range(NB):
                pe.wait_ge(z_ok, (n + 1) * TPB)
                for c in range(TPB):
                    last = nc.tensor.transpose(ps[:, n, c * P:(c + 1) * P], z_sb[:, n * TPB + c, :], id_f[:])
                last.then_inc(zT, 1)
            pe.wait_ge(col_ok, 1)
            pe.wait_ge(dch, 6)
            for n in range(NB):
                pe.wait_ge(hT_ok, n + 1)
                for c in range(TPB):
                    t = n * TPB + c
                    dst = ps[:, 4 + n, c * D:(c + 1) * D]
                    mm(dst, hT[:, t * P:(t + 1) * P], w_sb[:, 4, :], start=True, stop=False)
                    last = mm(dst, ones_row[:], b_row[0:1, 4, :], start=False, stop=True)
                last.then_inc(vproj, 1)
            for i in range(2 * NB):
                qk, n = i // NB, i % NB
                if i >= 2:
                    pe.wait_ge(rope, i - 1)
                for r in range(2):
                    last = mm(ps[:, 2 * (i % 2) + r, :], w_sb[:, 2 * qk + r, :], hT[:, n * BANK:(n + 1) * BANK],
                              start=True, stop=True)
                last.then_inc(proj, 1)

            def score(b, k, j, n, prev):
                if prev is not None:
                    pe.wait_ge(m_done, prev)
                mm(ps[:, MB + n % RING, :], m_q[0:SCORE_ROWS, b, k * P:(k + 1) * P],
                   m_k[0:SCORE_ROWS, b, j * BANK:(j + 1) * BANK], start=True, stop=True).then_inc(m_full, 1)

            def shift_transpose(h, read=True):
                pe.wait_ge(m_ready, h + 1)
                if read:
                    pe.wait_ge(ctx_ok, h - 1)
                nc.tensor.transpose(ps[:, AUX, 0:P // 2].bitcast(BF16), m_split[:], id_b[:]).then_inc(mT_mm, 1)

            def sums_transpose(h):
                pe.wait_ge(cx_ok, h + 1)
                pe.wait_ge(mT_ok, h + 2)
                for c in range(TPB):
                    last = nc.tensor.transpose(ps[:, AUX, c * P:(c + 1) * P], cx[:, c * P:(c + 1) * P], id_f[:])
                last.then_inc(cxT, 1)

            pe.wait_ge(pad_ok, 9)
            pe.wait_ge(v_ok, NB)
            pe.wait_ge(rope, 2 * NB)
            pe.wait_ge(ach, 1)
            for m in range(PRO):
                if m % NT == 0:
                    pe.wait_ge(setm[m // NT], SET)
                for j in range(NB):
                    n = NB * m + j
                    score(m // NT, m % NT, j, n, n - RING + 1 if n >= RING else None)
                if m == NT + 2:
                    shift_transpose(0, read=False)

            def values(step, k):
                b = (k // NT) % 2
                kt = k % NT
                pe.wait_ge(p_done, (step + 1) * NB)
                for j in range(NB):
                    last = mm(ps[32 * j:32 * j + 32, ACC, :], v_head[:, b, kt, :],
                              probs[:, k % PSLOTS, j * BANK:(j + 1) * BANK], start=(kt == 0), stop=(kt == NT - 1))
                last.then_inc(pv_done, 1)

            def pair(p, first=False, last=False):
                for k in range(PAIR):
                    m = k + PRO
                    b = k // NT
                    if k % NT == 0:
                        pe.wait_ge(sete[b], SET * (p + 1))
                        pe.wait_ge(shift[b], 16 * (p + 1))
                    do_max = not last or m < PAIR
                    if do_max and m % NT == 0:
                        pe.wait_ge(setm[(m // NT) % 2], SET * (p + m // PAIR + 1))
                    for j in range(NB):
                        q = NB * k + j
                        if not first or q >= RING:
                            pe.wait_ge(p_done, p * PAIR * NB + previous(q) + 1)
                        mm(ps[:, EB + q % RING, :], e_k[:, b, (k % NT) * P:(k % NT + 1) * P],
                           e_q[:, b, j * BANK:(j + 1) * BANK], start=True, stop=True).then_inc(s_full, 1)
                        if do_max:
                            score((m // NT) % 2, m % NT, j, q, (p * PAIR + PRO) * NB + previous(q) + 1)
                    if k == 0:
                        if not first:
                            values(p * PAIR - 1, PAIR - 1)
                    else:
                        if (k - 1) % NT == 0:
                            pe.wait_ge(vh_ok, 2 * p + b + 1)
                            if not first or b == 1:
                                pe.wait_ge(cx_ok, 2 * p + b)
                        values(p * PAIR + k - 1, k - 1)
                    if k % NT == 2 and not (first and k == 2):
                        sums_transpose(2 * p + b - 1)
                    if k % NT == NT - 3 and not (last and b == 1):
                        shift_transpose(2 * p + b + 1, read=not first or b == 1)

            pair(0, first=True)
            with pe.Fori(1, H // 2 - 1) as p:
                pair(p)
            pair(H // 2 - 1, last=True)
            values(H * NT - 1, PAIR - 1)
            pe.wait_ge(cx_ok, H)
            pe.wait_ge(ctx_ok, H - 1)
            for cc in range(TPB):
                lastmm = nc.tensor.transpose(ps[:, AUX, cc * P:(cc + 1) * P], cx[:, cc * P:(cc + 1) * P], id_f[:])
            lastmm.then_inc(cxT, 1)

            for n in range(NB):
                pe.wait_ge(z2_ok, (n + 1) * TPB)
                for cc in range(TPB):
                    lastmm = nc.tensor.transpose(ps[:, n, cc * P:(cc + 1) * P], z_sb[:, n * TPB + cc, :], id_f[:])
                lastmm.then_inc(zT2, 1)
            pe.wait_ge(hT2_ok, NB)
            for t in range(NT):
                lastmm = mm(ps[:, 7, t * E:(t + 1) * E], hT[:, t * P:(t + 1) * P], wr_sb[:], start=True, stop=True)
            lastmm.then_inc(log_mm, 1)

            def down(n):
                pe.wait_ge(h_ok, n + 1)
                if n >= 2:
                    pe.wait_ge(comb_ok, TPB * (n - 1))
                for cc in range(TPB):
                    lastmm = mm(ps[:, 4 + n % 2, cc * D:(cc + 1) * D], hh[n % 2][:, cc * P:(cc + 1) * P],
                                wd_sb[:, n % E, :], start=True, stop=True)
                lastmm.then_inc(down_mm, 1)

            for n in range(NB * E):
                e, col = n % E, slice((n // E) * BANK, (n // E + 1) * BANK)
                if n >= 2:
                    pe.wait_ge(h_ok, n - 1)
                mm(ps[:, 2 * (n % 2), :], wg_sb[:, e, :], hT[:, col], start=True, stop=True)
                mm(ps[:, 2 * (n % 2) + 1, :], wu_sb[:, e, :], hT[:, col], start=True, stop=True).then_inc(gu_mm, 1)
                if n >= 1:
                    down(n - 1)
            down(NB * E - 1)


_INS = ["L0_attn_hidden_states", "L0_attn_Wq", "L0_attn_bq", "L0_attn_Wk", "L0_attn_bk", "L0_attn_Wv", "L0_attn_bv",
        "L0_ffn_Wg", "L0_ffn_Wu", "L0_ffn_Wd", "L0_ffn_Wr", "L0_ffn_temperature", "L0_c", "L0_wmod"]


def tables():
    pos = np.arange(S, dtype=np.float32)
    inv = np.power(10000.0, -2.0 * np.arange(HD // 2) / HD).astype(np.float32)
    ang = (pos[None, :] * np.repeat(inv, 2)[:, None]).astype(np.float32).astype(np.float64)
    cos_t = np.tile(np.cos(ang), (H, 1)).astype(np.float32)
    sin_t = np.tile(np.sin(ang), (H, 1)).astype(np.float32)
    before = np.tril(np.ones((E, E), np.float32), -1)
    return {"cos": cos_t, "sin": sin_t, "ident": np.eye(P, dtype=np.float32),
            "tri": np.broadcast_to(before, (P, E, E)).copy()}


def kernel(**inputs):
    import concourse.bacc as bacc
    from concourse.bass_utils import run_bass_kernel_spmd

    nc = bacc.Bacc("TRN2", target_bir_lowering=False, num_devices=1)
    arrays, args = {}, []
    for name, a in [(n, np.ascontiguousarray(inputs[n])) for n in _INS] + list(tables().items()):
        arrays[f"in_{name}_dram"] = a
        args.append(nc.dram_tensor(f"in_{name}_dram", a.shape, mybir.dt.from_np(a.dtype), kind="ExternalInput").ap())
    args.append(nc.dram_tensor("out_0_dram", (1, S, D), F32, kind="ExternalOutput").ap())
    adaln_block(nc, *args)
    r = run_bass_kernel_spmd(nc, [arrays], core_ids=[0])
    return r.results[0]["out_0_dram"]
```

```python
from contextlib import ExitStack

import numpy as np

import concourse.bass as bass
from concourse import mybir

F32 = mybir.dt.float32
BF16 = mybir.dt.bfloat16
ACT = mybir.ActivationFunctionType
ALU = mybir.AluOpType
AX_X = mybir.AxisListType.X

P = 128
D = 128
S = 2048
H = 16
HD = D // H
NT = S // P
BANK = 512
NB = S // BANK
TPB = BANK // P
E = 8
EI = 128
EPS = 1e-5
SCALE = 1.0 / float(np.sqrt(np.float32(HD)))

SPLITS = 3
BLOCK = HD * SPLITS
ROWS = BLOCK * SPLITS
SHIFT_ROW = 96
SCORE_ROWS = SHIFT_ROW
LEAD = 3
PRO = NT + LEAD
PAIR = 2 * NT
EB, MB, ACC, AUX = 0, 3, 6, 7
RING = 3
OFF = (PAIR - PRO) * 4 % RING
PSLOTS = 4
MOPS = 4


def previous(k):
    return k - RING if k >= RING else {0: -2, 1: -1, 2: -3}[k]


def adaln_block(nc, x, wq, bq, wk, bk, wv, bv, wg, wu, wd, wr, temp, c, wmod, cos_t, sin_t, ident, tri, out):
    with ExitStack() as ctx:
        def sb(name, shape, dt=F32):
            return ctx.enter_context(nc.sbuf_tensor(name, shape, dt))

        def sem(name):
            return ctx.enter_context(nc.semaphore(name))

        split_dram = nc.dram_tensor("qk_split_scratch", [2, D, SPLITS, S], BF16).ap()
        ps = ctx.enter_context(nc.psum_tensor("ps", [P, 8, BANK], F32))

        x_sb = sb("x_sb", [P, NT, D])
        w_sb = sb("w_sb", [P, 5, D])
        b_row = sb("b_row", [1, 4, D])
        bv_all = sb("bv_all", [P, D])
        b_col = sb("b_col", [P, 4])
        id_f = sb("id_f", [P, P])
        id_b = sb("id_b", [P, P], BF16)
        ones_row = sb("ones_row", [1, P])
        wmod_sb = sb("wmod_sb", [P, 6 * D])
        cs = sb("cs", [P, 8])
        silu_b = sb("silu_b", [P, P])
        mod = sb("mod", [P, 6])
        gate_raw = sb("gate_raw", [P, 2, D])
        gate_sgn = sb("gate_sgn", [P, 2, D])
        gate_abs = sb("gate_abs", [P, 2, D])
        gate = sb("gate", [P, 2, D])
        wg_sb = sb("wg_sb", [P, E, EI])
        wu_sb = sb("wu_sb", [P, E, EI])
        wd_sb = sb("wd_sb", [P, E, D])
        wr_sb = sb("wr_sb", [P, E])
        temp_sb = sb("temp_sb", [P, 2])
        tri_sb = sb("tri_sb", [P, E, E])

        stats = sb("stats", [P, NT, 6])
        mv = sb("mv", [P, NT, 2])
        var_e = sb("var_e", [P, NT])
        mhalf = sb("mhalf", [P, NT])
        rstd = sb("rstd", [P, NT])
        z_sb = sb("z_sb", [P, NT, D])
        hT = sb("hT", [P, S])

        v_sb = sb("v_sb", [P, NT, D])
        parts = sb("parts", [P, 2, SPLITS, S], BF16)
        m_q = sb("m_q", [P, 2, S], BF16)
        m_k = sb("m_k", [P, 2, S], BF16)
        e_q = sb("e_q", [P, 2, S], BF16)
        e_k = sb("e_k", [P, 2, S], BF16)
        probs = sb("probs", [P, PSLOTS, S])
        v_head = sb("v_head", [P, 2, NT, 32])
        m_part = sb("m_part", [P, 2, NT, NB])
        m_neg = sb("m_neg", [P, NT])
        m_rest = sb("m_rest", [P, NT])
        m_split = sb("m_split", [P, P], BF16)
        mT = sb("mT", [SPLITS * NT, P], BF16)
        cx = sb("cx", [P, BANK])
        rsum = sb("rsum", [P, TPB, NB])
        ctx_sb = sb("ctx_sb", [P, NT, D])

        cos_sb, sin_sb = probs[:, 0, :], probs[:, 1, :]
        qk_f = probs[:, 2, :]
        qk_t = probs[:, 3, :]

        rt = sb("rt", [P, 14, NT * E])
        cmp = sb("cmp", [P, 2, NT * E * E])
        rs2 = sb("rs2", [P, 8, NT])
        sg = [probs[:, 0, i * BANK:(i + 1) * BANK] for i in range(2)]
        hh = [probs[:, 1, i * BANK:(i + 1) * BANK] for i in range(2)]
        y_sb = probs[:, 2, :].rearrange("p (t d) -> p t d", d=D)
        o_sb = probs[:, 3, :].rearrange("p (t d) -> p t d", d=D)

        x_in = [sem(f"x_in{n}") for n in range(NB)]
        w_in = sem("w_in")
        b_in = sem("b_in")
        c_in = sem("c_in")
        mod_in = sem("mod_in")
        t_in = sem("t_in")
        f_in = sem("f_in")
        id_in = sem("id_in")
        ones = sem("ones")
        dch = sem("dch")
        id_ok = sem("id_ok")
        rsum_ok = sem("rsum_ok")
        stat_ok = sem("stat_ok")
        rstd_ok = sem("rstd_ok")
        z_ok = sem("z_ok")
        zT = sem("zT")
        hT_ok = sem("hT_ok")
        w_rot = sem("w_rot")
        col_mm = sem("col_mm")
        col_ok = sem("col_ok")
        mod_mm = sem("mod_mm")
        mod_ok = sem("mod_ok")
        silu_ok = sem("silu_ok")
        e1 = sem("e1")
        proj = sem("proj")
        rope = sem("rope")
        part1 = sem("part1")
        rest1 = sem("rest1")
        part2 = sem("part2")
        part3 = sem("part3")
        split_out = sem("split_out")
        vproj = sem("vproj")
        v_ok = sem("v_ok")
        bv_in = sem("bv_in")
        vb_ok = sem("vb_ok")
        pad_ok = sem("pad_ok")
        s_full = sem("s_full")
        p_done = sem("p_done")
        m_full = sem("m_full")
        m_done = sem("m_done")
        pv_done = sem("pv_done")
        m_ready = sem("m_ready")
        mT_mm = sem("mT_mm")
        mT_ok = sem("mT_ok")
        cx_ok = sem("cx_ok")
        cxT = sem("cxT")
        ctx_ok = sem("ctx_ok")
        vh_ok = sem("vh_ok")
        stat2_ok = sem("stat2_ok")
        rstd2_ok = sem("rstd2_ok")
        z2_ok = sem("z2_ok")
        zT2 = sem("zT2")
        hT2_ok = sem("hT2_ok")
        log_mm = sem("log_mm")
        sig_in = sem("sig_in")
        sig_e = sem("sig_e")
        wexp_in = sem("wexp_in")
        wexp = sem("wexp")
        gu_mm = sem("gu_mm")
        silu_done = sem("silu_done")
        h_ok = sem("h_ok")
        down_mm = sem("down_mm")
        comb_ok = sem("comb_ok")
        y_ok = sem("y_ok")
        out_ok = sem("out_ok")
        setm = [sem("setm0"), sem("setm1")]
        sete = [sem("sete0"), sem("sete1")]
        shift = [sem("shift0"), sem("shift1")]

        block = ctx.enter_context(nc.Block())

        def operand_rows(sp, dst_q, dst_k, b, h, done):
            h8 = h * HD
            qs = split_dram[0, bass.ds(h8, HD)] if not isinstance(h, int) else split_dram[0, h8:h8 + HD]
            ks = split_dram[1, bass.ds(h8, HD)] if not isinstance(h, int) else split_dram[1, h8:h8 + HD]
            for i in range(SPLITS):
                rows = slice(i * BLOCK, (i + 1) * BLOCK)
                sp.dma_start(dst_q[rows, b, :],
                             qs[:, i:i + 1, :].broadcast_to([HD, SPLITS, S])).then_inc(done, 16)
                sp.dma_start(dst_k[rows, b, :], ks.rearrange("d j n -> (d j) n")).then_inc(done, 16)

        SET = 2 * SPLITS * 16

        @block.sync
        def _(sp):
            for i in range(4):
                t = slice(i * TPB, (i + 1) * TPB)
                sp.dma_start(x_sb[:, t, :], x[0].rearrange("(t p) d -> p t d", p=P)[:, t, :]).then_inc(x_in[i], 16)
            sp.dma_start(cos_sb, cos_t).then_inc(t_in, 16)
            sp.dma_start(sin_sb, sin_t).then_inc(t_in, 16)
            sp.dma_start(wg_sb[:], wg.rearrange("e d i -> d e i")).then_inc(f_in, 16)
            sp.dma_start(wu_sb[:], wu.rearrange("e d i -> d e i")).then_inc(f_in, 16)
            sp.dma_start(wd_sb[:], wd.rearrange("e i d -> i e d")).then_inc(f_in, 16)
            sp.dma_start(wr_sb[:], wr).then_inc(f_in, 16)
            sp.dma_start(temp_sb[:, 0:1], temp.rearrange("(a b) -> a b", a=1).broadcast_to([P, 1])).then_inc(f_in, 16)
            sp.dma_start(tri_sb[:], tri).then_inc(f_in, 16)
            for i in range(2 * NB):
                qk, col = i // NB, slice((i % NB) * BANK, (i % NB + 1) * BANK)
                sp.wait_ge(part1, i + 1)
                sp.wait_ge(part2, i + 1)
                sp.wait_ge(part3, i + 1)
                sp.dma_start(split_dram[qk, :, :, col], parts[:, qk, :, col]).then_inc(split_out, 16)
            sp.wait_ge(split_out, 16 * 2 * NB)
            sp.wait_ge(pad_ok, 9)
            operand_rows(sp, m_q, m_k, 0, 0, setm[0])
            operand_rows(sp, m_q, m_k, 1, 1, setm[1])
            operand_rows(sp, e_q, e_k, 0, 0, sete[0])

            def shift_rows(h, b):
                sp.wait_ge(mT_ok, h + 1)
                sp.dma_start(e_q[SHIFT_ROW:SHIFT_ROW + SPLITS, b, :].rearrange("i (t p) -> i t p", p=P),
                             mT[:]).then_inc(shift[b], 16)

            shift_rows(0, 0)

            def pair(p, first=False, last=False):
                if not last:
                    sp.wait_ge(m_done, (2 * p + 1) * NT * NB)
                    operand_rows(sp, m_q, m_k, 0, 2 * p + 2, setm[0])
                if not first:
                    sp.wait_ge(pv_done, 2 * p * NT)
                operand_rows(sp, e_q, e_k, 1, 2 * p + 1, sete[1])
                shift_rows(2 * p + 1, 1)
                if not last:
                    sp.wait_ge(m_done, (2 * p + 2) * NT * NB)
                    operand_rows(sp, m_q, m_k, 1, 2 * p + 3, setm[1])
                    sp.wait_ge(pv_done, (2 * p + 1) * NT)
                    operand_rows(sp, e_q, e_k, 0, 2 * p + 2, sete[0])
                    shift_rows(2 * p + 2, 0)

            pair(0, first=True)
            with sp.Fori(1, H // 2 - 1) as p:
                pair(p)
            pair(H // 2 - 1, last=True)
            sp.wait_ge(out_ok, NB)
            for i in range(NB):
                t = slice(i * TPB, (i + 1) * TPB)
                sp.dma_start(out[0].rearrange("(t p) d -> p t d", p=P)[:, t, :], o_sb[:, t, :]).then_inc(y_ok, 16)
            sp.wait_ge(y_ok, 16 * NB)

        @block.gpsimd
        def _(pool):
            nc.gpsimd.memset(mhalf[:], -0.5).then_inc(pad_ok, 1)
            pool.wait_ge(pad_ok, 1)
            for n in range(NB):
                t = slice(n * TPB, (n + 1) * TPB)
                pool.wait_ge(stat_ok, n + 1)
                nc.gpsimd.tensor_tensor(rstd[:, t], var_e[:, t], mhalf[:, t], ALU.pow).then_inc(rstd_ok, 1)
                pool.wait_ge(rstd_ok, n + 1)
            pads = [(m_q[64:96, :, :].bitcast(F32), 0.0), (m_k[64:96, :, :].bitcast(F32), 0.0),
                    (e_q[64:128, :, :].bitcast(F32), 0.0), (e_k[64:128, :, :].bitcast(F32), 0.0),
                    (e_k[SHIFT_ROW:SHIFT_ROW + SPLITS, :, :], 1.0),
                    (m_split[:], 0.0), (v_head[:], 0.0), (v_head[:, :, :, HD:HD + 1], 1.0)]
            for n, (buf, value) in enumerate(pads):
                nc.gpsimd.memset(buf, value).then_inc(pad_ok, 1)
                pool.wait_ge(pad_ok, n + 2)
            for i in range(2 * NB):
                qk, col = i // NB, slice((i % NB) * BANK, (i % NB + 1) * BANK)
                pool.wait_ge(part2, i + 1)
                nc.gpsimd.tensor_tensor(parts[:, qk, 2, col], qk_t[:, col], parts[:, qk, 1, col],
                                        ALU.subtract).then_inc(part3, 1)
            pool.wait_ge(bv_in, 16)
            for n in range(NB):
                t = slice(n * TPB, (n + 1) * TPB)
                pool.wait_ge(v_ok, n + 1)
                nc.gpsimd.tensor_tensor(v_sb[:, t, :], v_sb[:, t, :],
                                        bv_all[:].unsqueeze(1).broadcast_to([P, TPB, D]), ALU.add).then_inc(vb_ok, 1)
            pool.wait_ge(vb_ok, NB)

            def pair(p, first=False, last=False):
                for b in range(2):
                    h = 2 * p + b
                    if not first:
                        pool.wait_ge(pv_done, (h - 1) * NT)
                    src = v_sb[:, :, h * HD:(h + 1) * HD] if isinstance(h, int) else v_sb[:, :, bass.ds(h * HD, HD)]
                    nc.gpsimd.tensor_copy(v_head[:, b, :, 0:HD], src).then_inc(vh_ok, 1)

            pair(0, first=True)
            with pool.Fori(1, H // 2 - 1) as p:
                pair(p)
            pair(H // 2 - 1, last=True)
            for n in range(NB):
                t = slice(n * TPB, (n + 1) * TPB)
                pool.wait_ge(stat2_ok, n + 1)
                nc.gpsimd.tensor_tensor(rstd[:, t], var_e[:, t], mhalf[:, t], ALU.pow).then_inc(rstd2_ok, 1)

        @block.scalar
        def _(act):
            act.dma_start(cs[:, 0:1], c.rearrange("a d -> d a")).then_inc(c_in, 16)
            for i, b in ((0, bq), (2, bk)):
                act.dma_start(b_row[0:1, i, :], b.rearrange("(a d) -> a d", a=1)).then_inc(b_in, 16)
            for i, w in ((0, wq), (2, wk)):
                act.dma_start(w_sb[:, i, :], w).then_inc(w_in, 16)
            act.dma_start(id_f[:], ident).then_inc(id_in, 16)
            act.dma_start(wmod_sb[:], wmod).then_inc(mod_in, 16)
            act.dma_start(w_sb[:, 4, :], wv).then_inc(w_in, 16)
            act.dma_start(bv_all[:], bv.rearrange("(a d) -> a d", a=1).broadcast_to([P, D])).then_inc(bv_in, 16)
            act.wait_ge(c_in, 16)
            nc.scalar.activation(cs[:, 1:2], cs[:, 0:1], ACT.Exp, scale=-1.0).then_inc(e1, 1)
            act.wait_ge(id_in, 16)
            nc.scalar.copy(id_b[:], id_f[:]).then_inc(id_ok, 1)
            act.wait_ge(mod_ok, 1)
            for n in range(NB):
                act.wait_ge(zT, n + 1)
                nc.scalar.activation(hT[:, n * BANK:(n + 1) * BANK], ps[:, n, :], ACT.Identity,
                                     bias=mod[:, 0:1], scale=mod[:, 1:2]).then_inc(hT_ok, 1)
            def values_copy(n):
                act.wait_ge(vproj, n + 1)
                nc.scalar.copy(v_sb[:, n * TPB:(n + 1) * TPB, :],
                               ps[:, 4 + n % 2, :].rearrange("p (t d) -> p t d", d=D)).then_inc(v_ok, 1)

            def second_part(i):
                qk, col = i // NB, slice((i % NB) * BANK, (i % NB + 1) * BANK)
                act.wait_ge(rest1, i + 1)
                nc.scalar.copy(parts[:, qk, 1, col], qk_t[:, col]).then_inc(part2, 1)

            for i in range(2 * NB):
                qk, col = i // NB, slice((i % NB) * BANK, (i % NB + 1) * BANK)
                act.wait_ge(rope, i + 1)
                nc.scalar.copy(parts[:, qk, 0, col], qk_f[:, col]).then_inc(part1, 1)
                if i >= 1:
                    second_part(i - 1)
                if i % 2 == 0 and i >= 2:
                    values_copy(i // 2 - 1)
            second_part(2 * NB - 1)
            values_copy(NB - 1)

            def shift_copy(h):
                act.wait_ge(mT_mm, h + 1)
                nc.scalar.copy(mT[:], ps[0:SPLITS * NT, AUX, 0:P // 2].bitcast(BF16)).then_inc(mT_ok, 1)

            act.wait_ge(part3, 2 * NB)
            shift_copy(0)

            def pair(p, first=False, last=False):
                for k in range(PAIR):
                    step = p * PAIR + k
                    if k % NT == NT - 1 and not (last and k > NT):
                        b = 1 if k < NT else 0
                        h = 2 * p + (1 if k < NT else 2)
                        act.wait_ge(mT_mm, h + 1)
                        act.wait_ge(shift[1 - b], 16 * (p + 1))
                        nc.scalar.copy(mT[:], ps[0:SPLITS * NT, AUX, 0:P // 2].bitcast(BF16)).then_inc(mT_ok, 1)
                    if not first or k >= PSLOTS:
                        act.wait_ge(pv_done, step - PSLOTS + 1)
                    for j in range(NB):
                        q = 4 * k + j
                        act.wait_ge(s_full, p * PAIR * NB + q + 1)
                        nc.scalar.activation(probs[:, k % PSLOTS, j * BANK:(j + 1) * BANK],
                                             ps[:, EB + q % RING, :], ACT.Exp, scale=SCALE).then_inc(p_done, 1)
                    if k % NT == 0 and not (first and k == 0):
                        h = 2 * p + k // NT - 1
                        act.wait_ge(pv_done, (h + 1) * NT)
                        if not first:
                            act.wait_ge(cxT, h)
                        nc.scalar.copy(cx[:], ps[:, ACC, :]).then_inc(cx_ok, 1)

            pair(0, first=True)
            with act.Fori(1, H // 2 - 1) as p:
                pair(p)
            pair(H // 2 - 1, last=True)
            act.wait_ge(pv_done, H * NT)
            act.wait_ge(cxT, H - 1)
            nc.scalar.copy(cx[:], ps[:, ACC, :]).then_inc(cx_ok, 1)

            def second_norm(n):
                act.wait_ge(zT2, n + 1)
                nc.scalar.activation(hT[:, n * BANK:(n + 1) * BANK], ps[:, ACC + n % 2, :], ACT.Identity,
                                     bias=mod[:, 3:4], scale=mod[:, 4:5]).then_inc(hT2_ok, 1)

            def silu(n):
                act.wait_ge(gu_mm, n + 1)
                if n >= 2:
                    act.wait_ge(h_ok, n - 1)
                nc.scalar.activation(sg[n % 2], ps[:, 2 * (n % 2), :], ACT.Silu).then_inc(silu_done, 1)

            second_norm(0)
            silu(0)
            second_norm(1)
            silu(1)
            second_norm(2)
            second_norm(3)
            act.wait_ge(sig_in, 1)
            nc.scalar.activation(rt[:, 1], rt[:, 0], ACT.Exp).then_inc(sig_e, 1)
            act.wait_ge(wexp_in, 1)
            nc.scalar.activation(rt[:, 5], rt[:, 4], ACT.Exp, scale=-1.0 / 0.1).then_inc(wexp, 1)
            nc.scalar.activation(rt[:, 6], rt[:, 4], ACT.Exp, scale=-1.0 / 0.3).then_inc(wexp, 1)
            for n in range(2, NB * E):
                silu(n)

        @block.vector
        def _(dve):
            count = [0]

            def link(ins):
                count[0] += 1
                ins.then_inc(dch, 1)
                dve.wait_ge(dch, count[0])

            nc.vector.memset(ones_row[:], 1.0).then_inc(ones, 1)

            def statistics(n, done):
                for t in range(n * TPB, (n + 1) * TPB):
                    ins = nc.vector.bn_stats(stats[:, t, :], x_sb[:, t, :])
                link(ins)
                for t in range(n * TPB, (n + 1) * TPB):
                    ins = nc.vector.bn_aggr(mv[:, t, :], stats[:, t, :])
                link(ins)
                t = slice(n * TPB, (n + 1) * TPB)
                nc.vector.tensor_scalar(var_e[:, t], mv[:, t, 1], EPS, None, ALU.add).then_inc(done, 1)

            def standard(n, done):
                for t in range(n * TPB, (n + 1) * TPB):
                    nc.vector.tensor_scalar(z_sb[:, t, :], x_sb[:, t, :], mv[:, t, 0:1], rstd[:, t:t + 1],
                                            ALU.subtract, ALU.mult).then_inc(done, 1)

            for n in range(NB):
                dve.wait_ge(x_in[n], 16)
                statistics(n, stat_ok)
            dve.wait_ge(e1, 1)
            link(nc.vector.tensor_scalar(cs[:, 2:3], cs[:, 1:2], 1.0, None, ALU.add))
            link(nc.vector.reciprocal(cs[:, 3:4], cs[:, 2:3]))
            link(nc.vector.tensor_tensor(cs[:, 4:5], cs[:, 0:1], cs[:, 3:4], ALU.mult))
            nc.vector.tensor_copy(silu_b[:], cs[:, 4:5].broadcast_to([P, P])).then_inc(silu_ok, 1)
            dve.wait_ge(w_in, 48)
            dve.wait_ge(b_in, 32)
            for i in (0, 2):
                for src, dst in ((w_sb[:, i, :], w_sb[:, i + 1, :]), (b_row[0:1, i, :], b_row[0:1, i + 1, :])):
                    sv = src.rearrange("p (m e) -> p m e", e=2)
                    dv = dst.rearrange("p (m e) -> p m e", e=2)
                    nc.vector.tensor_scalar(dv[:, :, 0], sv[:, :, 1], -1.0, None, ALU.mult).then_inc(w_rot, 1)
                    nc.vector.tensor_copy(dv[:, :, 1], sv[:, :, 0]).then_inc(w_rot, 1)
            for n in range(NB):
                dve.wait_ge(rstd_ok, n + 1)
                standard(n, z_ok)
                if n == 0:
                    dve.wait_ge(mod_mm, 1)
                    link(nc.vector.tensor_copy(mod[:], ps[:, 7, 2 * D:2 * D + 6]))
                    scales = mod[:].rearrange("p (a b) -> p a b", b=3)[:, :, 1]
                    nc.vector.tensor_scalar(scales, scales, 1.0, None, ALU.add).then_inc(mod_ok, 1)
            dve.wait_ge(col_mm, 1)
            nc.vector.tensor_copy(b_col[:], ps[:, 6, 0:4]).then_inc(col_ok, 1)
            dve.wait_ge(col_ok, 1)

            def first_rest(i):
                qk, col = i // NB, slice((i % NB) * BANK, (i % NB + 1) * BANK)
                dve.wait_ge(part1, i + 1)
                nc.vector.tensor_tensor(qk_t[:, col], qk_f[:, col], parts[:, qk, 0, col],
                                        ALU.subtract).then_inc(rest1, 1)

            dve.wait_ge(t_in, 32)
            for i in range(2 * NB):
                qk, n = i // NB, i % NB
                col = slice(n * BANK, (n + 1) * BANK)
                bank = 2 * (i % 2)
                dve.wait_ge(proj, i + 1)
                if i >= NB:
                    dve.wait_ge(part2, i - NB + 1)
                    dve.wait_ge(part3, i - NB + 1)
                nc.vector.scalar_tensor_tensor(qk_f[:, col], ps[:, bank, :], b_col[:, 2 * qk:2 * qk + 1],
                                               cos_sb[:, col], ALU.add, ALU.mult).then_inc(dch, 1)
                count[0] += 1
                link(nc.vector.scalar_tensor_tensor(qk_t[:, col], ps[:, bank + 1, :], b_col[:, 2 * qk + 1:2 * qk + 2],
                                                    sin_sb[:, col], ALU.add, ALU.mult))
                nc.vector.tensor_tensor(qk_f[:, col], qk_f[:, col], qk_t[:, col], ALU.add).then_inc(rope, 1)
                if i >= 1:
                    first_rest(i - 1)
            first_rest(2 * NB - 1)

            link(nc.vector.tensor_copy(gate_raw[:], ps[:, 7, 0:2 * D].rearrange("p (a d) -> p a d", a=2)))
            link(nc.vector.tensor_scalar(gate_abs[:], gate_raw[:], -1.0, None, ALU.mult))
            link(nc.vector.tensor_tensor(gate_abs[:], gate_abs[:], gate_raw[:], ALU.max))
            link(nc.vector.tensor_scalar(gate_abs[:], gate_abs[:], 0.25, None, ALU.max))
            link(nc.vector.tensor_scalar(gate_sgn[:], gate_raw[:], 0.0, 2.0, ALU.is_ge, ALU.mult))
            link(nc.vector.tensor_scalar(gate_sgn[:], gate_sgn[:], -1.0, None, ALU.add))
            link(nc.vector.tensor_tensor(gate[:], gate_sgn[:], gate_abs[:], ALU.mult))

            base = count[0]

            def chain(ins, h, n):
                ins.then_inc(dch, 1)
                dve.wait_ge(dch, base + h * MOPS + n + 1)

            def max_step(m, b, k, before):
                for j in range(NB):
                    dve.wait_ge(m_full, m * NB + j + 1)
                    nc.vector.tensor_reduce(m_part[:, b, k % NT, j:j + 1], ps[:, MB + (before + j) % RING, :],
                                            AX_X, ALU.max).then_inc(m_done, 1)

            def max_head(h, b, first=False):
                dve.wait_ge(m_done, (h + 1) * NT * NB)
                if not first:
                    dve.wait_ge(mT_mm, h)
                chain(nc.vector.tensor_reduce(m_neg[:], m_part[:, b], AX_X, ALU.max, negate=True), h, 0)
                chain(nc.vector.tensor_copy(m_split[:, 0:NT], m_neg[:]), h, 1)
                chain(nc.vector.tensor_tensor(m_rest[:], m_neg[:], m_split[:, 0:NT], ALU.subtract), h, 2)
                chain(nc.vector.tensor_copy(m_split[:, NT:2 * NT], m_rest[:]), h, 3)
                nc.vector.tensor_tensor(m_split[:, 2 * NT:3 * NT], m_rest[:], m_split[:, NT:2 * NT],
                                        ALU.subtract).then_inc(m_ready, 1)

            def normalise(h):
                dve.wait_ge(cxT, h + 1)
                aux = ps[:, AUX, :].rearrange("p (c j r) -> p c j r", c=TPB, r=32)
                nc.vector.reciprocal(rsum[:], aux[:, :, :, HD]).then_inc(rsum_ok, 1)
                dve.wait_ge(rsum_ok, h + 1)
                dst = ctx_sb[:, :, h * HD:(h + 1) * HD] if isinstance(h, int) else ctx_sb[:, :, bass.ds(h * HD, HD)]
                nc.vector.tensor_tensor(dst.rearrange("p (j c) d -> p c j d", c=TPB), aux[:, :, :, 0:HD],
                                        rsum[:].unsqueeze(3).broadcast_to([P, TPB, NB, HD]),
                                        ALU.mult).then_inc(ctx_ok, 1)

            dve.wait_ge(pad_ok, 9)
            for m in range(PRO):
                max_step(m, m // NT, m, NB * m + OFF)
                if m == NT - 1:
                    max_head(0, 0, first=True)

            def pair(p, first=False, last=False):
                for k in range(PAIR):
                    m = k + PRO
                    if not last or m < PAIR:
                        max_step(p * PAIR + m, (m // NT) % 2, m, NB * k)
                        if m % NT == NT - 1:
                            max_head(2 * p + m // NT, (m // NT) % 2)
                    if k % NT == 2 and not (first and k == 2):
                        normalise(2 * p + k // NT - 1)

            pair(0, first=True)
            with dve.Fori(1, H // 2 - 1) as p:
                pair(p)
            pair(H // 2 - 1, last=True)
            normalise(H - 1)
            count[0] = base + H * MOPS

            dve.wait_ge(ctx_ok, H)
            for n in range(NB):
                t = slice(n * TPB, (n + 1) * TPB)
                link(nc.vector.tensor_tensor(ctx_sb[:, t], ctx_sb[:, t], gate[:, 0:1, :].broadcast_to([P, TPB, D]),
                                             ALU.mult))
                link(nc.vector.tensor_tensor(x_sb[:, t], x_sb[:, t], ctx_sb[:, t], ALU.add))
                statistics(n, stat2_ok)
                if n >= 1:
                    dve.wait_ge(rstd2_ok, n)
                    standard(n - 1, z2_ok)
            dve.wait_ge(rstd2_ok, NB)
            standard(NB - 1, z2_ok)

            def hidden(n):
                dve.wait_ge(silu_done, n + 1)
                if n >= 2:
                    dve.wait_ge(down_mm, n - 1)
                nc.vector.tensor_tensor(hh[n % 2], sg[n % 2], ps[:, 2 * (n % 2) + 1, :], ALU.mult).then_inc(h_ok, 1)

            hidden(0)
            hidden(1)
            dve.wait_ge(f_in, 96)
            link(nc.vector.reciprocal(temp_sb[:, 1:2], temp_sb[:, 0:1]))

            def te(i):
                return rt[:, i].rearrange("p (t e) -> p t e", e=E)

            def wide(a):
                return a.unsqueeze(2).broadcast_to([P, NT, E])

            dve.wait_ge(log_mm, 1)
            nc.vector.tensor_scalar(rt[:, 0], ps[:, ACC, 0:NT * E], temp_sb[:, 1:2], -1.0, ALU.mult,
                                    ALU.mult).then_inc(sig_in, 1)
            dve.wait_ge(sig_e, 1)
            link(nc.vector.tensor_scalar(rt[:, 2], rt[:, 1], 1.0, None, ALU.add))
            link(nc.vector.reciprocal(rt[:, 3], rt[:, 2]))
            lower = float(0.5 - np.log(4.0 / 3.0))
            center = float(1.0 / np.e)
            link(nc.vector.tensor_scalar(rt[:, 0], rt[:, 3], -center, None, ALU.add))
            link(nc.vector.tensor_scalar(rt[:, 1], rt[:, 0], -1.0, None, ALU.mult))
            nc.vector.tensor_tensor(rt[:, 4], rt[:, 0], rt[:, 1], ALU.max).then_inc(wexp_in, 1)
            link(nc.vector.tensor_scalar(rt[:, 7], rt[:, 3], lower, None, ALU.is_ge))
            link(nc.vector.tensor_scalar(rt[:, 8], rt[:, 3], 0.5, None, ALU.is_le))
            link(nc.vector.tensor_tensor(rt[:, 7], rt[:, 7], rt[:, 8], ALU.mult))
            dve.wait_ge(wexp, 2)
            link(nc.vector.tensor_tensor(rt[:, 9], rt[:, 5], rt[:, 7], ALU.mult))
            link(nc.vector.tensor_reduce(rs2[:, 0], te(9), AX_X, ALU.add))
            link(nc.vector.tensor_scalar(rs2[:, 1], rs2[:, 0], 1e-8, None, ALU.is_lt))
            link(nc.vector.tensor_scalar(rs2[:, 2], rs2[:, 1], -1.0, 1.0, ALU.mult, ALU.add))
            mine = te(6).unsqueeze(3).broadcast_to([P, NT, E, E])
            other = te(6).unsqueeze(2).broadcast_to([P, NT, E, E])
            cm = [cmp[:, i].rearrange("p (t a b) -> p t a b", a=E, b=E) for i in range(2)]
            link(nc.vector.tensor_tensor(cm[0], other, mine, ALU.is_gt))
            link(nc.vector.tensor_tensor(cm[1], other, mine, ALU.is_equal))
            link(nc.vector.tensor_tensor(cm[1], cm[1], tri_sb[:].unsqueeze(1).broadcast_to([P, NT, E, E]), ALU.mult))
            link(nc.vector.tensor_tensor(cmp[:, 0], cmp[:, 0], cmp[:, 1], ALU.add))
            link(nc.vector.tensor_reduce(rt[:, 10], cmp[:, 0].rearrange("p (t b) -> p t b", b=E), AX_X, ALU.add))
            link(nc.vector.tensor_scalar(rt[:, 11], rt[:, 10], 2.0, None, ALU.is_lt))
            link(nc.vector.tensor_tensor(rt[:, 11], rt[:, 11], rt[:, 6], ALU.mult))
            link(nc.vector.tensor_reduce(rs2[:, 3], te(11), AX_X, ALU.add))
            link(nc.vector.tensor_scalar(rs2[:, 3], rs2[:, 3], 1e-8, None, ALU.max))
            link(nc.vector.reciprocal(rs2[:, 4], rs2[:, 3]))
            link(nc.vector.tensor_tensor(te(11), te(11), wide(rs2[:, 4]), ALU.mult))
            link(nc.vector.tensor_tensor(te(11), te(11), wide(rs2[:, 1]), ALU.mult))
            link(nc.vector.tensor_tensor(te(9), te(9), wide(rs2[:, 2]), ALU.mult))
            link(nc.vector.tensor_tensor(rt[:, 9], rt[:, 9], rt[:, 11], ALU.add))
            link(nc.vector.tensor_reduce(rs2[:, 5], te(9), AX_X, ALU.add))
            link(nc.vector.tensor_scalar(rs2[:, 5], rs2[:, 5], 1e-8, None, ALU.max))
            link(nc.vector.reciprocal(rs2[:, 6], rs2[:, 5]))
            link(nc.vector.tensor_tensor(te(12), te(9), wide(rs2[:, 6]), ALU.mult))

            def combine(n):
                dve.wait_ge(down_mm, n + 1)
                if n >= 1:
                    dve.wait_ge(comb_ok, TPB * n)
                e, tb = n % E, n // E
                for c in range(TPB):
                    t = tb * TPB + c
                    src = ps[:, 4 + n % 2, c * D:(c + 1) * D]
                    wt = te(12)[:, t, e:e + 1]
                    if e == 0:
                        last = nc.vector.tensor_scalar(y_sb[:, t, :], src, wt, None, ALU.mult)
                    else:
                        last = nc.vector.scalar_tensor_tensor(y_sb[:, t, :], src, wt, y_sb[:, t, :], ALU.mult, ALU.add)
                    last.then_inc(comb_ok, 1)
                if e == E - 1:
                    dve.wait_ge(comb_ok, TPB * (n + 1))
                    t = slice(tb * TPB, (tb + 1) * TPB)
                    link(nc.vector.tensor_tensor(y_sb[:, t, :], y_sb[:, t, :],
                                                 gate[:, 1:2, :].broadcast_to([P, TPB, D]), ALU.mult))
                    nc.vector.tensor_tensor(o_sb[:, t, :], x_sb[:, t, :], y_sb[:, t, :], ALU.add).then_inc(out_ok, 1)

            combine(0)
            for n in range(2, NB * E):
                hidden(n)
                combine(n - 1)
            combine(NB * E - 1)

        @block.tensor
        def _(pe):
            mm = nc.tensor.matmul
            pe.wait_ge(id_in, 16)
            pe.wait_ge(silu_ok, 1)
            pe.wait_ge(mod_in, 16)
            for i in range(6):
                mm(ps[:, 7, 2 * D + i:2 * D + i + 1], wmod_sb[:, i * D:(i + 1) * D], cs[:, 4:5], start=True, stop=True)
            for i, g in enumerate((2, 5)):
                last = mm(ps[:, 7, i * D:(i + 1) * D], silu_b[:], wmod_sb[:, g * D:(g + 1) * D], start=True, stop=True)
            last.then_inc(mod_mm, 1)
            for n in range(NB):
                pe.wait_ge(z_ok, (n + 1) * TPB)
                for c in range(TPB):
                    last = nc.tensor.transpose(ps[:, n, c * P:(c + 1) * P], z_sb[:, n * TPB + c, :], id_f[:])
                last.then_inc(zT, 1)
            pe.wait_ge(w_rot, 8)
            pe.wait_ge(ones, 1)
            for i in range(4):
                last = mm(ps[:, 6, i:i + 1], b_row[0:1, i, :], ones_row[0:1, 0:1], start=True, stop=True)
            last.then_inc(col_mm, 1)

            def project_values(n):
                if n >= 2:
                    pe.wait_ge(v_ok, n - 1)
                for c in range(TPB):
                    t = n * TPB + c
                    last = mm(ps[:, 4 + n % 2, c * D:(c + 1) * D], hT[:, t * P:(t + 1) * P], w_sb[:, 4, :],
                              start=True, stop=True)
                last.then_inc(vproj, 1)

            for i in range(2 * NB):
                qk, n = i // NB, i % NB
                pe.wait_ge(hT_ok, min(2 * i + 2, NB))
                if i >= 2:
                    pe.wait_ge(rope, i - 1)
                for r in range(2):
                    last = mm(ps[:, 2 * (i % 2) + r, :], w_sb[:, 2 * qk + r, :], hT[:, n * BANK:(n + 1) * BANK],
                              start=True, stop=True)
                last.then_inc(proj, 1)
                if i % 2 == 1:
                    project_values(i // 2)

            def score(b, k, j, n, prev):
                if prev is not None:
                    pe.wait_ge(m_done, prev)
                mm(ps[:, MB + n % RING, :], m_q[0:SCORE_ROWS, b, k * P:(k + 1) * P],
                   m_k[0:SCORE_ROWS, b, j * BANK:(j + 1) * BANK], start=True, stop=True).then_inc(m_full, 1)

            def shift_transpose(h, read=True):
                pe.wait_ge(m_ready, h + 1)
                if read:
                    pe.wait_ge(ctx_ok, h - 1)
                nc.tensor.transpose(ps[:, AUX, 0:P // 2].bitcast(BF16), m_split[:], id_b[:]).then_inc(mT_mm, 1)

            def sums_transpose(h):
                pe.wait_ge(cx_ok, h + 1)
                pe.wait_ge(mT_ok, h + 2)
                for c in range(TPB):
                    last = nc.tensor.transpose(ps[:, AUX, c * P:(c + 1) * P], cx[:, c * P:(c + 1) * P], id_f[:])
                last.then_inc(cxT, 1)

            pe.wait_ge(pad_ok, 9)
            pe.wait_ge(v_ok, NB)
            pe.wait_ge(rope, 2 * NB)
            pe.wait_ge(id_ok, 1)
            for m in range(PRO):
                if m % NT == 0:
                    pe.wait_ge(setm[m // NT], SET)
                for j in range(NB):
                    n = NB * m + j
                    score(m // NT, m % NT, j, n + OFF, n - RING + 1 if n >= RING else None)
                if m == NT:
                    shift_transpose(0, read=False)

            def values(step, k):
                b = (k // NT) % 2
                kt = k % NT
                pe.wait_ge(p_done, (step + 1) * NB)
                for j in range(NB):
                    last = mm(ps[32 * j:32 * j + 32, ACC, :], v_head[:, b, kt, :],
                              probs[:, k % PSLOTS, j * BANK:(j + 1) * BANK], start=(kt == 0), stop=(kt == NT - 1))
                last.then_inc(pv_done, 1)

            def pair(p, first=False, last=False):
                for k in range(PAIR):
                    m = k + PRO
                    b = k // NT
                    if k % NT == 0:
                        pe.wait_ge(sete[b], SET * (p + 1))
                        pe.wait_ge(shift[b], 16 * (p + 1))
                    do_max = not last or m < PAIR
                    if do_max and m % NT == 0:
                        pe.wait_ge(setm[(m // NT) % 2], SET * (p + m // PAIR + 1))
                    for j in range(NB):
                        q = NB * k + j
                        if not first or q >= RING:
                            pe.wait_ge(p_done, p * PAIR * NB + previous(q) + 1)
                        mm(ps[:, EB + q % RING, :], e_k[:, b, (k % NT) * P:(k % NT + 1) * P],
                           e_q[:, b, j * BANK:(j + 1) * BANK], start=True, stop=True).then_inc(s_full, 1)
                        if do_max:
                            score((m // NT) % 2, m % NT, j, q, (p * PAIR + PRO) * NB + previous(q) + 1)
                    if k == 0:
                        if not first:
                            values(p * PAIR - 1, PAIR - 1)
                    else:
                        if (k - 1) % NT == 0:
                            pe.wait_ge(vh_ok, 2 * p + b + 1)
                            if not first or b == 1:
                                pe.wait_ge(cx_ok, 2 * p + b)
                        values(p * PAIR + k - 1, k - 1)
                    if k % NT == 2 and not (first and k == 2):
                        sums_transpose(2 * p + b - 1)
                    if k % NT == NT - 2 and not (last and b == 1):
                        shift_transpose(2 * p + b + 1, read=not first or b == 1)

            pair(0, first=True)
            with pe.Fori(1, H // 2 - 1) as p:
                pair(p)
            pair(H // 2 - 1, last=True)
            values(H * NT - 1, PAIR - 1)
            pe.wait_ge(cx_ok, H)
            pe.wait_ge(ctx_ok, H - 1)
            for cc in range(TPB):
                lastmm = nc.tensor.transpose(ps[:, AUX, cc * P:(cc + 1) * P], cx[:, cc * P:(cc + 1) * P], id_f[:])
            lastmm.then_inc(cxT, 1)

            def second_transpose(n):
                pe.wait_ge(z2_ok, (n + 1) * TPB)
                if n >= 2:
                    pe.wait_ge(hT2_ok, n - 1)
                for cc in range(TPB):
                    lastmm = nc.tensor.transpose(ps[:, ACC + n % 2, cc * P:(cc + 1) * P], z_sb[:, n * TPB + cc, :], id_f[:])
                lastmm.then_inc(zT2, 1)

            def gate_up(n):
                e, col = n % E, slice((n // E) * BANK, (n // E + 1) * BANK)
                pe.wait_ge(hT2_ok, n // E + 1)
                if n >= 2:
                    pe.wait_ge(h_ok, n - 1)
                mm(ps[:, 2 * (n % 2), :], wg_sb[:, e, :], hT[:, col], start=True, stop=True)
                mm(ps[:, 2 * (n % 2) + 1, :], wu_sb[:, e, :], hT[:, col], start=True, stop=True).then_inc(gu_mm, 1)

            def down(n):
                pe.wait_ge(h_ok, n + 1)
                if n >= 2:
                    pe.wait_ge(comb_ok, TPB * (n - 1))
                for cc in range(TPB):
                    lastmm = mm(ps[:, 4 + n % 2, cc * D:(cc + 1) * D], hh[n % 2][:, cc * P:(cc + 1) * P],
                                wd_sb[:, n % E, :], start=True, stop=True)
                lastmm.then_inc(down_mm, 1)

            pe.wait_ge(f_in, 96)
            second_transpose(0)
            gate_up(0)
            second_transpose(1)
            gate_up(1)
            second_transpose(2)
            second_transpose(3)
            pe.wait_ge(hT2_ok, NB)
            for t in range(NT):
                lastmm = mm(ps[:, ACC, t * E:(t + 1) * E], hT[:, t * P:(t + 1) * P], wr_sb[:], start=True, stop=True)
            lastmm.then_inc(log_mm, 1)
            down(0)
            for n in range(2, NB * E):
                gate_up(n)
                down(n - 1)
            down(NB * E - 1)


_INS = ["L0_attn_hidden_states", "L0_attn_Wq", "L0_attn_bq", "L0_attn_Wk", "L0_attn_bk", "L0_attn_Wv", "L0_attn_bv",
        "L0_ffn_Wg", "L0_ffn_Wu", "L0_ffn_Wd", "L0_ffn_Wr", "L0_ffn_temperature", "L0_c", "L0_wmod"]


def tables():
    pos = np.arange(S, dtype=np.float32)
    inv = np.power(10000.0, -2.0 * np.arange(HD // 2) / HD).astype(np.float32)
    ang = (pos[None, :] * np.repeat(inv, 2)[:, None]).astype(np.float32).astype(np.float64)
    cos_t = np.tile(np.cos(ang), (H, 1)).astype(np.float32)
    sin_t = np.tile(np.sin(ang), (H, 1)).astype(np.float32)
    before = np.tril(np.ones((E, E), np.float32), -1)
    return {"cos": cos_t, "sin": sin_t, "ident": np.eye(P, dtype=np.float32),
            "tri": np.broadcast_to(before, (P, E, E)).copy()}


def kernel(**inputs):
    import concourse.bacc as bacc
    from concourse.bass_utils import run_bass_kernel_spmd

    nc = bacc.Bacc("TRN2", target_bir_lowering=False, num_devices=1)
    arrays, args = {}, []
    for name, a in [(n, np.ascontiguousarray(inputs[n])) for n in _INS] + list(tables().items()):
        arrays[f"in_{name}_dram"] = a
        args.append(nc.dram_tensor(f"in_{name}_dram", a.shape, mybir.dt.from_np(a.dtype), kind="ExternalInput").ap())
    args.append(nc.dram_tensor("out_0_dram", (1, S, D), F32, kind="ExternalOutput").ap())
    adaln_block(nc, *args)
    r = run_bass_kernel_spmd(nc, [arrays], core_ids=[0])
    return r.results[0]["out_0_dram"]
```

```python
from contextlib import ExitStack

import numpy as np

import concourse.bass as bass
from concourse import mybir

F32 = mybir.dt.float32
BF16 = mybir.dt.bfloat16
ACT = mybir.ActivationFunctionType
ALU = mybir.AluOpType
AX_X = mybir.AxisListType.X

P = 128
D = 128
S = 2048
H = 16
HD = D // H
NT = S // P
BANK = 512
NB = S // BANK
TPB = BANK // P
E = 8
EI = 128
EPS = 1e-5
SCALE = 1.0 / float(np.sqrt(np.float32(HD)))

SPLITS = 3
BLOCK = HD * SPLITS
SHIFT_ROW = 96
SCORE_ROWS = SHIFT_ROW
LEAD = 3
PRO = NT + LEAD
PAIR = 2 * NT
EB, MB, ACC, AUX = 0, 3, 6, 7
RING = 3
WIDE = 6
PRO_OFF = 2
EARLY = 5
FIRST_MAX = ([(m, 0) for m in range(EARLY)] + [(m, 2) for m in range(EARLY)] +
             [(m, j) for m in range(EARLY, PRO) for j in (0, 2)])
LONE = (2 * NT - PRO) * NB
POOL_RESTS = 6
ZT2 = 4
DOWN = (4, 5, 7, 6)
PSLOTS = 4
MOPS = 4


def previous(k):
    return k - RING if k >= RING else {0: -2, 1: -1, 2: -3}[k]


def exp_bank(q, last):
    return EB + ((q - LONE) % WIDE if last and q >= LONE else q % RING)


def adaln_block(nc, x, wq, bq, wk, bk, wv, bv, wg, wu, wd, wr, temp, c, wmod, cos_t, sin_t, ident, rank, out):
    with ExitStack() as ctx:
        def sb(name, shape, dt=F32):
            return ctx.enter_context(nc.sbuf_tensor(name, shape, dt))

        def sem(name):
            return ctx.enter_context(nc.semaphore(name))

        split_dram = nc.dram_tensor("qk_split_scratch", [2, D, SPLITS, S], BF16).ap()
        ps = ctx.enter_context(nc.psum_tensor("ps", [P, 8, BANK], F32))

        x_sb = sb("x_sb", [P, NT, D])
        w_sb = sb("w_sb", [P, 5, D])
        b_row = sb("b_row", [1, 4, D])
        bv_all = sb("bv_all", [P, D])
        b_col = sb("b_col", [P, 4])
        id_f = sb("id_f", [P, P])
        id_b = sb("id_b", [P, P], BF16)
        ones_row = sb("ones_row", [1, P])
        wmod_sb = sb("wmod_sb", [P, 6 * D])
        cs = sb("cs", [P, 8])
        silu_b = sb("silu_b", [P, P])
        mod = sb("mod", [P, 6])
        gate_raw = sb("gate_raw", [P, 2, D])
        gate_sgn = sb("gate_sgn", [P, 2, D])
        gate_abs = sb("gate_abs", [P, 2, D])
        gate = sb("gate", [P, 2, D])
        wg_sb = sb("wg_sb", [P, E, EI])
        wu_sb = sb("wu_sb", [P, E, EI])
        wd_sb = sb("wd_sb", [P, E, D])
        wr_sb = sb("wr_sb", [P, E])
        temp_sb = sb("temp_sb", [P, 2])
        rank_sb = sb("rank_sb", [P, E])

        stats = sb("stats", [P, NT, 6])
        mv = sb("mv", [P, NT, 2])
        var_e = sb("var_e", [P, NT])
        mhalf = sb("mhalf", [P, NT])
        rstd = sb("rstd", [P, NT])
        neg_mean = sb("neg_mean", [P, NT])
        z_bias = sb("z_bias", [P, NT])
        z_sb = sb("z_sb", [P, NT, D])
        hT = sb("hT", [P, S])

        v_sb = sb("v_sb", [P, NT, D])
        parts = sb("parts", [P, 2, SPLITS, S], BF16)
        m_q = sb("m_q", [P, 2, S], BF16)
        m_k = sb("m_k", [P, 2, S], BF16)
        e_q = sb("e_q", [P, 2, S], BF16)
        e_k = sb("e_k", [P, 2, S], BF16)
        probs = sb("probs", [P, PSLOTS, S])
        v_head = sb("v_head", [P, 2, NT, 32])
        m_part = sb("m_part", [P, 2, NT, NB])
        m_neg = sb("m_neg", [P, NT])
        m_rest = sb("m_rest", [P, NT])
        m_split = sb("m_split", [P, P], BF16)
        mT = sb("mT", [SPLITS * NT, P], BF16)
        cx = sb("cx", [P, BANK])
        rsum = sb("rsum", [P, TPB, NB])
        ctx_sb = sb("ctx_sb", [P, NT, D])

        cos_sb, sin_sb = probs[:, 0, :], probs[:, 1, :]
        qk_f = probs[:, 2, :]
        qk_t = probs[:, 3, :]

        rt = sb("rt", [P, 18, NT * E])
        rs2 = sb("rs2", [P, 8, NT])
        sg = [probs[:, 0, i * BANK:(i + 1) * BANK] for i in range(2)]
        hh = [probs[:, 1, i * BANK:(i + 1) * BANK] for i in range(2)]
        o_flat = probs[:, 3, :]
        o_sb = o_flat.rearrange("p (t d) -> p t d", d=D)
        x_flat = x_sb[:].rearrange("p t d -> p (t d)")

        x_in = [sem(f"x_in{n}") for n in range(NB)]
        w_in = sem("w_in")
        wv_in = sem("wv_in")
        b_in = sem("b_in")
        c_in = sem("c_in")
        mod_in = sem("mod_in")
        t_in = sem("t_in")
        f_in = sem("f_in")
        wd_in = sem("wd_in")
        wd_ok = sem("wd_ok")
        id_in = sem("id_in")
        ones = sem("ones")
        dch = sem("dch")
        id_ok = sem("id_ok")
        rsum_ok = sem("rsum_ok")
        stat_ok = sem("stat_ok")
        rstd_ok = sem("rstd_ok")
        bias_ok = sem("bias_ok")
        za_ok = sem("za_ok")
        z_ok = sem("z_ok")
        zT = sem("zT")
        hT_ok = sem("hT_ok")
        w_rot = sem("w_rot")
        col_mm = sem("col_mm")
        col_ok = sem("col_ok")
        mod_mm = sem("mod_mm")
        mod_ok = sem("mod_ok")
        silu_ok = sem("silu_ok")
        e1 = sem("e1")
        proj = sem("proj")
        rope = sem("rope")
        part1 = sem("part1")
        rest1 = sem("rest1")
        rest1_pool = sem("rest1_pool")
        part2 = sem("part2")
        part3 = sem("part3")
        split_out = [sem("q_out"), sem("k_half_out"), sem("k_rest_out")]
        vproj = sem("vproj")
        v_ok = sem("v_ok")
        bv_in = sem("bv_in")
        vb_ok = sem("vb_ok")
        gate_ok = sem("gate_ok")
        x1_ok = sem("x1_ok")
        pad_ok = sem("pad_ok")
        s_full = sem("s_full")
        p_done = sem("p_done")
        m_full = sem("m_full")
        m_done = sem("m_done")
        pv_done = sem("pv_done")
        m_ready = sem("m_ready")
        mT_mm = sem("mT_mm")
        mT_ok = sem("mT_ok")
        cx_ok = sem("cx_ok")
        cxT = sem("cxT")
        ctx_ok = sem("ctx_ok")
        vh_ok = sem("vh_ok")
        stat2_ok = sem("stat2_ok")
        rstd2_ok = sem("rstd2_ok")
        bias2_ok = sem("bias2_ok")
        za2_ok = sem("za2_ok")
        z2_ok = sem("z2_ok")
        zT2 = sem("zT2")
        hT2_ok = sem("hT2_ok")
        log_mm = sem("log_mm")
        sig_in = sem("sig_in")
        sig_e = sem("sig_e")
        wexp_in = sem("wexp_in")
        wexp = sem("wexp")
        gu_mm = sem("gu_mm")
        silu_done = sem("silu_done")
        h_ok = sem("h_ok")
        down_mm = sem("down_mm")
        comb_ok = sem("comb_ok")
        y_ok = sem("y_ok")
        half_in = sem("half_in")
        rest_in = sem("rest_in")
        setm = [sem("setm0"), sem("setm1")]
        sete = [sem("sete0"), sem("sete1")]
        shift = [sem("shift0"), sem("shift1")]

        block = ctx.enter_context(nc.Block())

        def query_rows(sp, dst, b, h, done):
            rows_of = slice(h * HD, (h + 1) * HD) if isinstance(h, int) else bass.ds(h * HD, HD)
            qs = split_dram[0, rows_of]
            for i in range(SPLITS):
                sp.dma_start(dst[i * BLOCK:(i + 1) * BLOCK, b, :],
                             qs[:, i:i + 1, :].broadcast_to([HD, SPLITS, S])).then_inc(done, 16)

        def key_rows(sp, dst, b, h, done, col=slice(0, S)):
            rows_of = slice(h * HD, (h + 1) * HD) if isinstance(h, int) else bass.ds(h * HD, HD)
            ks = split_dram[1, rows_of].rearrange("d j n -> (d j) n")
            for i in range(SPLITS):
                sp.dma_start(dst[i * BLOCK:(i + 1) * BLOCK, b, col], ks[:, col]).then_inc(done, 16)

        def operand_rows(sp, dst_q, dst_k, b, h, done):
            query_rows(sp, dst_q, b, h, done)
            key_rows(sp, dst_k, b, h, done)

        SET = 2 * SPLITS * 16

        @block.sync
        def _(sp):
            for i in range(4):
                t = slice(i * TPB, (i + 1) * TPB)
                sp.dma_start(x_sb[:, t, :], x[0].rearrange("(t p) d -> p t d", p=P)[:, t, :]).then_inc(x_in[i], 16)
            for i in range(2 * NB):
                qk, col = i // NB, slice((i % NB) * BANK, (i % NB + 1) * BANK)
                sp.wait_ge(part1, i + 1)
                sp.wait_ge(part2, i + 1)
                sp.wait_ge(part3, i + 1)
                written = split_out[(i >= NB) + (i >= 3 * NB // 2)]
                sp.dma_start(split_dram[qk, :, :, col], parts[:, qk, :, col]).then_inc(written, 16)
                if i == NB + 1:
                    sp.wait_ge(split_out[0], 16 * NB)
                    sp.wait_ge(pad_ok, 3)
                    query_rows(sp, m_q, 0, 0, half_in)
                if i == 3 * NB // 2:
                    sp.wait_ge(split_out[1], 16 * NB // 2)
                    key_rows(sp, m_k, 0, 0, half_in, slice(0, S // 2))
            sp.wait_ge(split_out[2], 16 * NB // 2)
            key_rows(sp, m_k, 0, 0, rest_in, slice(S // 2, S))
            query_rows(sp, m_q, 1, 1, setm[1])
            key_rows(sp, m_k, 1, 1, setm[1])
            sp.wait_ge(pad_ok, 7)
            query_rows(sp, e_q, 0, 0, sete[0])
            key_rows(sp, e_k, 0, 0, sete[0])

            def shift_rows(h, b):
                sp.wait_ge(mT_ok, h + 1)
                sp.dma_start(e_q[SHIFT_ROW:SHIFT_ROW + SPLITS, b, :].rearrange("i (t p) -> i t p", p=P),
                             mT[:]).then_inc(shift[b], 16)

            sp.dma_start(wg_sb[:], wg.rearrange("e d i -> d e i")).then_inc(f_in, 16)
            sp.dma_start(wu_sb[:], wu.rearrange("e d i -> d e i")).then_inc(f_in, 16)
            sp.dma_start(wd_sb[:], wd.rearrange("e i d -> i e d")).then_inc(wd_in, 16)
            sp.dma_start(wr_sb[:], wr).then_inc(f_in, 16)
            sp.dma_start(temp_sb[:, 0:1], temp.rearrange("(a b) -> a b", a=1).broadcast_to([P, 1])).then_inc(f_in, 16)
            sp.dma_start(rank_sb[:], rank).then_inc(f_in, 16)
            shift_rows(0, 0)

            def pair(p, first=False, last=False):
                if not last:
                    sp.wait_ge(m_done, (2 * p + 1) * NT * NB)
                    operand_rows(sp, m_q, m_k, 0, 2 * p + 2, setm[0])
                if not first:
                    sp.wait_ge(pv_done, 2 * p * NT)
                operand_rows(sp, e_q, e_k, 1, 2 * p + 1, sete[1])
                shift_rows(2 * p + 1, 1)
                if not last:
                    sp.wait_ge(m_done, (2 * p + 2) * NT * NB)
                    operand_rows(sp, m_q, m_k, 1, 2 * p + 3, setm[1])
                    sp.wait_ge(pv_done, (2 * p + 1) * NT)
                    operand_rows(sp, e_q, e_k, 0, 2 * p + 2, sete[0])
                    shift_rows(2 * p + 2, 0)

            pair(0, first=True)
            with sp.Fori(1, H // 2 - 1) as p:
                pair(p)
            pair(H // 2 - 1, last=True)
            for i in range(NB):
                t = slice(i * TPB, (i + 1) * TPB)
                sp.wait_ge(comb_ok, TPB * E * (i + 1))
                sp.dma_start(out[0].rearrange("(t p) d -> p t d", p=P)[:, t, :], o_sb[:, t, :]).then_inc(y_ok, 16)
            sp.wait_ge(y_ok, 16 * NB)

        @block.gpsimd
        def _(pool):
            pads = [(mhalf[:], -0.5),
                    (m_q[64:96, :, :].bitcast(F32), 0.0), (m_k[64:96, :, :].bitcast(F32), 0.0),
                    (e_q[64:128, :, :].bitcast(F32), 0.0), (e_k[64:128, :, :].bitcast(F32), 0.0),
                    (e_k[SHIFT_ROW:SHIFT_ROW + SPLITS, :, :], 1.0),
                    (m_split[:], 0.0), (v_head[:], 0.0), (v_head[:, :, :, HD:HD + 1], 1.0)]

            def fill(first, end):
                for n in range(first, end):
                    nc.gpsimd.memset(*pads[n]).then_inc(pad_ok, 1)
                    pool.wait_ge(pad_ok, n + 1)

            fill(0, 3)
            for n in range(NB):
                t = slice(n * TPB, (n + 1) * TPB)
                pool.wait_ge(stat_ok, 2 * n + 2)
                nc.gpsimd.tensor_tensor(rstd[:, t], var_e[:, t], mhalf[:, t], ALU.pow).then_inc(rstd_ok, 1)
                pool.wait_ge(rstd_ok, n + 1)
                nc.gpsimd.tensor_tensor(z_bias[:, t], neg_mean[:, t], rstd[:, t], ALU.mult).then_inc(bias_ok, 1)
            pool.wait_ge(bias_ok, NB)
            pool.wait_ge(w_in, 32)
            pool.wait_ge(b_in, 32)
            for i in (0, 2):
                for src, dst in ((w_sb[:, i, :], w_sb[:, i + 1, :]), (b_row[0:1, i, :], b_row[0:1, i + 1, :])):
                    sv = src.rearrange("p (m e) -> p m e", e=2)
                    dv = dst.rearrange("p (m e) -> p m e", e=2)
                    nc.gpsimd.tensor_scalar(dv[:, :, 0], sv[:, :, 1], -1.0, None, ALU.mult).then_inc(w_rot, 1)
                    nc.gpsimd.tensor_copy(dv[:, :, 1], sv[:, :, 0]).then_inc(w_rot, 1)
            pool.wait_ge(w_rot, 8)

            def first_rest(i):
                qk, col = i // NB, slice((i % NB) * BANK, (i % NB + 1) * BANK)
                pool.wait_ge(part1, i + 1)
                nc.gpsimd.tensor_tensor(qk_t[:, col], qk_f[:, col], parts[:, qk, 0, col],
                                        ALU.subtract).then_inc(rest1_pool, 1)

            first_rest(0)
            for i in range(2 * NB):
                qk, col = i // NB, slice((i % NB) * BANK, (i % NB + 1) * BANK)
                if i + 1 < POOL_RESTS:
                    first_rest(i + 1)
                pool.wait_ge(part2, i + 1)
                nc.gpsimd.tensor_tensor(parts[:, qk, 2, col], qk_t[:, col], parts[:, qk, 1, col],
                                        ALU.subtract).then_inc(part3, 1)
            pool.wait_ge(part3, 2 * NB)
            fill(3, 9)
            pool.wait_ge(bv_in, 16)
            for n in range(NB):
                t = slice(n * TPB, (n + 1) * TPB)
                pool.wait_ge(v_ok, n + 1)
                nc.gpsimd.tensor_tensor(v_sb[:, t, :], v_sb[:, t, :],
                                        bv_all[:].unsqueeze(1).broadcast_to([P, TPB, D]), ALU.add).then_inc(vb_ok, 1)
            pool.wait_ge(vb_ok, NB)
            pool.wait_ge(gate_ok, 1)
            for n in range(NB):
                t = slice(n * TPB, (n + 1) * TPB)
                nc.gpsimd.tensor_tensor(v_sb[:, t, :], v_sb[:, t, :],
                                        gate[:, 0:1, :].broadcast_to([P, TPB, D]), ALU.mult).then_inc(vb_ok, 1)
            pool.wait_ge(vb_ok, 2 * NB)

            def head_values(h, b):
                v = v_sb[:, :, h * HD:(h + 1) * HD] if isinstance(h, int) else v_sb[:, :, bass.ds(h * HD, HD)]
                nc.gpsimd.tensor_copy(v_head[:, b, :, 0:HD], v).then_inc(vh_ok, 1)

            def add_context(h):
                pool.wait_ge(ctx_ok, h + 1)
                if isinstance(h, int):
                    xs, cs_ = x_sb[:, :, h * HD:(h + 1) * HD], ctx_sb[:, :, h * HD:(h + 1) * HD]
                else:
                    xs, cs_ = x_sb[:, :, bass.ds(h * HD, HD)], ctx_sb[:, :, bass.ds(h * HD, HD)]
                nc.gpsimd.tensor_tensor(xs, xs, cs_, ALU.add).then_inc(x1_ok, 1)

            head_values(0, 0)
            pool.wait_ge(wd_in, 16)
            for e in range(E):
                nc.gpsimd.tensor_tensor(wd_sb[:, e, :], wd_sb[:, e, :], gate[:, 1, :], ALU.mult).then_inc(wd_ok, 1)

            def pair(p, first=False, last=False):
                if not first:
                    pool.wait_ge(pv_done, 2 * p * NT)
                head_values(2 * p + 1, 1)
                if not first:
                    add_context(2 * p - 1)
                if not last:
                    pool.wait_ge(pv_done, (2 * p + 1) * NT)
                    head_values(2 * p + 2, 0)
                add_context(2 * p)

            pair(0, first=True)
            with pool.Fori(1, H // 2 - 1) as p:
                pair(p)
            pair(H // 2 - 1, last=True)
            add_context(H - 1)
            for n in range(NB):
                t = slice(n * TPB, (n + 1) * TPB)
                pool.wait_ge(stat2_ok, 2 * n + 2)
                nc.gpsimd.tensor_tensor(rstd[:, t], var_e[:, t], mhalf[:, t], ALU.pow).then_inc(rstd2_ok, 1)
                pool.wait_ge(rstd2_ok, n + 1)
                nc.gpsimd.tensor_tensor(z_bias[:, t], neg_mean[:, t], rstd[:, t], ALU.mult).then_inc(bias2_ok, 1)

        @block.scalar
        def _(act):
            act.dma_start(cs[:, 0:1], c.rearrange("a d -> d a")).then_inc(c_in, 16)
            act.dma_start(id_f[:], ident).then_inc(id_in, 16)
            act.dma_start(wmod_sb[:], wmod).then_inc(mod_in, 16)
            act.wait_ge(c_in, 16)
            nc.scalar.activation(cs[:, 1:2], cs[:, 0:1], ACT.Exp, scale=-1.0).then_inc(e1, 1)
            for i, b in ((0, bq), (2, bk)):
                act.dma_start(b_row[0:1, i, :], b.rearrange("(a d) -> a d", a=1)).then_inc(b_in, 16)
            for i, w in ((0, wq), (2, wk)):
                act.dma_start(w_sb[:, i, :], w).then_inc(w_in, 16)
            act.dma_start(w_sb[:, 4, :], wv).then_inc(wv_in, 16)
            act.dma_start(bv_all[:], bv.rearrange("(a d) -> a d", a=1).broadcast_to([P, D])).then_inc(bv_in, 16)
            act.dma_start(cos_sb, cos_t).then_inc(t_in, 16)
            act.dma_start(sin_sb, sin_t).then_inc(t_in, 16)
            act.wait_ge(id_in, 16)
            nc.scalar.copy(id_b[:], id_f[:]).then_inc(id_ok, 1)

            def standard(n, done):
                for t in range(n * TPB + TPB // 2, (n + 1) * TPB):
                    nc.scalar.activation(z_sb[:, t, :], x_sb[:, t, :], ACT.Identity,
                                         bias=z_bias[:, t:t + 1], scale=rstd[:, t:t + 1]).then_inc(done, 1)

            for n in range(NB):
                act.wait_ge(bias_ok, n + 1)
                standard(n, za_ok)
            act.wait_ge(mod_ok, 1)
            for n in range(NB):
                act.wait_ge(zT, n + 1)
                nc.scalar.activation(hT[:, n * BANK:(n + 1) * BANK], ps[:, n, :], ACT.Identity,
                                     bias=mod[:, 0:1], scale=mod[:, 1:2]).then_inc(hT_ok, 1)

            def values_copy(n):
                act.wait_ge(vproj, n + 1)
                nc.scalar.copy(v_sb[:, n * TPB:(n + 1) * TPB, :],
                               ps[:, 4 + n % 2, :].rearrange("p (t d) -> p t d", d=D)).then_inc(v_ok, 1)

            def second_part(i):
                qk, col = i // NB, slice((i % NB) * BANK, (i % NB + 1) * BANK)
                if i < POOL_RESTS:
                    act.wait_ge(rest1_pool, i + 1)
                else:
                    act.wait_ge(rest1, i - POOL_RESTS + 1)
                nc.scalar.copy(parts[:, qk, 1, col], qk_t[:, col]).then_inc(part2, 1)

            for i in range(2 * NB):
                qk, col = i // NB, slice((i % NB) * BANK, (i % NB + 1) * BANK)
                act.wait_ge(rope, i + 1)
                nc.scalar.copy(parts[:, qk, 0, col], qk_f[:, col]).then_inc(part1, 1)
                if i >= 1:
                    second_part(i - 1)
                if i % 2 == 0 and i >= 2:
                    values_copy(i // 2 - 1)
            second_part(2 * NB - 1)
            values_copy(NB - 1)

            def shift_copy(h):
                act.wait_ge(mT_mm, h + 1)
                nc.scalar.copy(mT[:], ps[0:SPLITS * NT, AUX, 0:P // 2].bitcast(BF16)).then_inc(mT_ok, 1)

            act.wait_ge(part3, 2 * NB)
            shift_copy(0)

            def pair(p, first=False, last=False):
                for k in range(PAIR):
                    step = p * PAIR + k
                    if not first or k >= PSLOTS:
                        act.wait_ge(pv_done, step - PSLOTS + 1)
                    for j in range(NB):
                        q = 4 * k + j
                        act.wait_ge(s_full, p * PAIR * NB + q + 1)
                        nc.scalar.activation(probs[:, k % PSLOTS, j * BANK:(j + 1) * BANK],
                                             ps[:, exp_bank(q, last), :], ACT.Exp, scale=SCALE).then_inc(p_done, 1)
                        if k % NT == NT - 2 and j == 1 and not (last and k > NT):
                            h = 2 * p + k // NT + 1
                            act.wait_ge(shift[k // NT], 16 * (p + 1))
                            shift_copy(h)
                    if k % NT == 0 and not (first and k == 0):
                        h = 2 * p + k // NT - 1
                        act.wait_ge(pv_done, (h + 1) * NT)
                        if not first:
                            act.wait_ge(cxT, h)
                        nc.scalar.copy(cx[:], ps[:, ACC, :]).then_inc(cx_ok, 1)

            pair(0, first=True)
            with act.Fori(1, H // 2 - 1) as p:
                pair(p)
            pair(H // 2 - 1, last=True)
            act.wait_ge(pv_done, H * NT)
            act.wait_ge(cxT, H - 1)
            nc.scalar.copy(cx[:], ps[:, ACC, :]).then_inc(cx_ok, 1)

            def second_norm(n):
                act.wait_ge(zT2, n + 1)
                nc.scalar.activation(hT[:, n * BANK:(n + 1) * BANK], ps[:, ZT2 + n % 2, :], ACT.Identity,
                                     bias=mod[:, 3:4], scale=mod[:, 4:5]).then_inc(hT2_ok, 1)

            def silu(tb, e):
                n = E * tb + e
                act.wait_ge(gu_mm, n + 1)
                if not (isinstance(tb, int) and n < 2):
                    act.wait_ge(h_ok, n - 1)
                nc.scalar.activation(sg[e % 2], ps[:, 2 * (e % 2), :], ACT.Silu).then_inc(silu_done, 1)

            for n in range(NB):
                act.wait_ge(bias2_ok, n + 1)
                standard(n, za2_ok)
                if n >= 1:
                    second_norm(n - 1)
            second_norm(NB - 1)
            act.wait_ge(sig_in, 1)
            nc.scalar.activation(rt[:, 1], rt[:, 0], ACT.Exp).then_inc(sig_e, 1)
            act.wait_ge(wexp_in, 1)
            nc.scalar.activation(rt[:, 5], rt[:, 4], ACT.Exp, scale=-1.0 / 0.1).then_inc(wexp, 1)
            nc.scalar.activation(rt[:, 6], rt[:, 4], ACT.Exp, scale=-1.0 / 0.3).then_inc(wexp, 1)
            for e in range(E):
                silu(0, e)
            with act.Fori(1, NB) as tb:
                for e in range(E):
                    silu(tb, e)

        @block.vector
        def _(dve):
            count = [0]

            def link(ins):
                count[0] += 1
                ins.then_inc(dch, 1)
                dve.wait_ge(dch, count[0])

            nc.vector.memset(ones_row[:], 1.0).then_inc(ones, 1)

            def statistics(n, done):
                for t in range(n * TPB, (n + 1) * TPB):
                    ins = nc.vector.bn_stats(stats[:, t, :], x_sb[:, t, :])
                link(ins)
                for t in range(n * TPB, (n + 1) * TPB):
                    ins = nc.vector.bn_aggr(mv[:, t, :], stats[:, t, :])
                link(ins)
                t = slice(n * TPB, (n + 1) * TPB)
                nc.vector.tensor_scalar(neg_mean[:, t], mv[:, t, 0], -1.0, None, ALU.mult).then_inc(done, 1)
                nc.vector.tensor_scalar(var_e[:, t], mv[:, t, 1], EPS, None, ALU.add).then_inc(done, 1)

            def standard(n, done):
                for t in range(n * TPB, n * TPB + TPB // 2):
                    nc.vector.tensor_scalar(z_sb[:, t, :], x_sb[:, t, :], mv[:, t, 0:1], rstd[:, t:t + 1],
                                            ALU.subtract, ALU.mult).then_inc(done, 1)

            for n in range(NB):
                dve.wait_ge(x_in[n], 16)
                statistics(n, stat_ok)
                if n != 1:
                    continue
                dve.wait_ge(e1, 1)
                link(nc.vector.tensor_scalar(cs[:, 2:3], cs[:, 1:2], 1.0, None, ALU.add))
                link(nc.vector.reciprocal(cs[:, 3:4], cs[:, 2:3]))
                link(nc.vector.tensor_tensor(cs[:, 4:5], cs[:, 0:1], cs[:, 3:4], ALU.mult))
                nc.vector.tensor_copy(silu_b[:], cs[:, 4:5].broadcast_to([P, P])).then_inc(silu_ok, 1)
            for n in range(NB):
                dve.wait_ge(rstd_ok, n + 1)
                standard(n, z_ok)
                if n == 0:
                    dve.wait_ge(mod_mm, 1)
                    link(nc.vector.tensor_copy(mod[:], ps[:, 7, 2 * D:2 * D + 6]))
                    scales = mod[:].rearrange("p (a b) -> p a b", b=3)[:, :, 1]
                    nc.vector.tensor_scalar(scales, scales, 1.0, None, ALU.add).then_inc(mod_ok, 1)
            dve.wait_ge(col_mm, 1)
            nc.vector.tensor_copy(b_col[:], ps[:, 6, 0:4]).then_inc(col_ok, 1)
            dve.wait_ge(col_ok, 1)

            def first_rest(i):
                if i < POOL_RESTS:
                    return
                qk, col = i // NB, slice((i % NB) * BANK, (i % NB + 1) * BANK)
                dve.wait_ge(part1, i + 1)
                nc.vector.tensor_tensor(qk_t[:, col], qk_f[:, col], parts[:, qk, 0, col],
                                        ALU.subtract).then_inc(rest1, 1)

            dve.wait_ge(t_in, 32)
            for i in range(2 * NB):
                qk, n = i // NB, i % NB
                col = slice(n * BANK, (n + 1) * BANK)
                bank = 2 * (i % 2)
                dve.wait_ge(proj, i + 1)
                if i >= NB:
                    dve.wait_ge(part2, i - NB + 1)
                    dve.wait_ge(part3, i - NB + 1)
                nc.vector.scalar_tensor_tensor(qk_f[:, col], ps[:, bank, :], b_col[:, 2 * qk:2 * qk + 1],
                                               cos_sb[:, col], ALU.add, ALU.mult).then_inc(dch, 1)
                count[0] += 1
                link(nc.vector.scalar_tensor_tensor(qk_t[:, col], ps[:, bank + 1, :], b_col[:, 2 * qk + 1:2 * qk + 2],
                                                    sin_sb[:, col], ALU.add, ALU.mult))
                nc.vector.tensor_tensor(qk_f[:, col], qk_f[:, col], qk_t[:, col], ALU.add).then_inc(rope, 1)
                if i >= 1:
                    first_rest(i - 1)
            first_rest(2 * NB - 1)

            link(nc.vector.tensor_copy(gate_raw[:], ps[:, 7, 0:2 * D].rearrange("p (a d) -> p a d", a=2)))
            link(nc.vector.tensor_scalar(gate_abs[:], gate_raw[:], -1.0, None, ALU.mult))
            link(nc.vector.tensor_tensor(gate_abs[:], gate_abs[:], gate_raw[:], ALU.max))
            link(nc.vector.tensor_scalar(gate_abs[:], gate_abs[:], 0.25, None, ALU.max))
            link(nc.vector.tensor_scalar(gate_sgn[:], gate_raw[:], 0.0, 2.0, ALU.is_ge, ALU.mult))
            link(nc.vector.tensor_scalar(gate_sgn[:], gate_sgn[:], -1.0, None, ALU.add))
            nc.vector.tensor_tensor(gate[:], gate_sgn[:], gate_abs[:], ALU.mult).then_inc(gate_ok, 1)

            base = count[0]

            def chain(ins, h, n):
                ins.then_inc(dch, 1)
                dve.wait_ge(dch, base + h * MOPS + n + 1)

            def max_step(m, b, k, before, between):
                for j in range(NB):
                    dve.wait_ge(m_full, m * NB + j + 1)
                    nc.vector.tensor_reduce(m_part[:, b, k % NT, j:j + 1], ps[:, MB + (before + j) % RING, :],
                                            AX_X, ALU.max).then_inc(m_done, 1)
                    if j in between:
                        between[j]()

            def max_head(h, b, first=False):
                def one():
                    dve.wait_ge(m_done, (h + 1) * NT * NB)
                    if not first:
                        dve.wait_ge(mT_mm, h)
                    chain(nc.vector.tensor_reduce(m_neg[:], m_part[:, b], AX_X, ALU.max, negate=True), h, 0)
                    nc.vector.tensor_copy(m_split[:, 0:NT], m_neg[:]).then_inc(dch, 1)

                def two():
                    dve.wait_ge(dch, base + h * MOPS + 2)
                    chain(nc.vector.tensor_tensor(m_rest[:], m_neg[:], m_split[:, 0:NT], ALU.subtract), h, 2)
                    nc.vector.tensor_copy(m_split[:, NT:2 * NT], m_rest[:]).then_inc(dch, 1)

                def three():
                    dve.wait_ge(dch, base + h * MOPS + 4)
                    nc.vector.tensor_tensor(m_split[:, 2 * NT:3 * NT], m_rest[:], m_split[:, NT:2 * NT],
                                            ALU.subtract).then_inc(m_ready, 1)
                return one, two, three

            def normalise(h):
                aux = ps[:, AUX, :].rearrange("p (c j r) -> p c j r", c=TPB, r=32)

                def one():
                    dve.wait_ge(cxT, h + 1)
                    nc.vector.reciprocal(rsum[:], aux[:, :, :, HD]).then_inc(rsum_ok, 1)

                def two():
                    dve.wait_ge(rsum_ok, h + 1)
                    dst = ctx_sb[:, :, h * HD:(h + 1) * HD] if isinstance(h, int) else \
                        ctx_sb[:, :, bass.ds(h * HD, HD)]
                    nc.vector.tensor_tensor(dst.rearrange("p (j c) d -> p c j d", c=TPB), aux[:, :, :, 0:HD],
                                            rsum[:].unsqueeze(3).broadcast_to([P, TPB, NB, HD]),
                                            ALU.mult).then_inc(ctx_ok, 1)
                return one, two

            for i, (m, j) in enumerate(FIRST_MAX):
                bank = (2 * i + PRO_OFF) % WIDE
                dve.wait_ge(m_full, 2 * i + 2)
                nc.vector.tensor_reduce(m_part[:, m // NT, m % NT, j:j + 2], ps[:, bank:bank + 2, :],
                                        AX_X, ALU.max).then_inc(m_done, 2)
                if (m, j) == (NT - 1, 2):
                    dve.wait_ge(pad_ok, 7)
                    for part in max_head(0, 0, first=True):
                        part()

            def pair(p, first=False, last=False):
                for k in range(PAIR):
                    m = k + PRO
                    between = {}
                    if m % NT == 0:
                        h = 2 * p + m // NT - 1
                        between = dict(enumerate(max_head(h, (m // NT + 1) % 2)))
                    if k % NT == 3 and not (first and k == 3):
                        between = dict(enumerate(normalise(2 * p + k // NT - 1)))
                    if not last or m < PAIR:
                        max_step(p * PAIR + m, (m // NT) % 2, m, NB * k, between)
                    elif m == PAIR or k % NT == 3:
                        for part in between.values():
                            part()

            pair(0, first=True)
            with dve.Fori(1, H // 2 - 1) as p:
                pair(p)
            pair(H // 2 - 1, last=True)
            for part in normalise(H - 1):
                part()
            count[0] = base + H * MOPS

            dve.wait_ge(gate_ok, 1)
            dve.wait_ge(x1_ok, H)
            for n in range(NB):
                statistics(n, stat2_ok)
                if n >= 1:
                    dve.wait_ge(rstd2_ok, n)
                    standard(n - 1, z2_ok)
            dve.wait_ge(rstd2_ok, NB)
            standard(NB - 1, z2_ok)

            def hidden(tb, e):
                n = E * tb + e
                dve.wait_ge(silu_done, n + 1)
                if not (isinstance(tb, int) and n < 2):
                    dve.wait_ge(down_mm, n - 1)
                nc.vector.tensor_tensor(hh[e % 2], sg[e % 2], ps[:, 2 * (e % 2) + 1, :], ALU.mult).then_inc(h_ok, 1)

            dve.wait_ge(f_in, 80)
            link(nc.vector.reciprocal(temp_sb[:, 1:2], temp_sb[:, 0:1]))

            def te(i):
                return rt[:, i].rearrange("p (t e) -> p t e", e=E)

            def wide(a):
                return a.unsqueeze(2).broadcast_to([P, NT, E])

            dve.wait_ge(log_mm, NB)
            nc.vector.tensor_scalar(rt[:, 0], ps[:, ACC, 0:NT * E], temp_sb[:, 1:2], -1.0, ALU.mult,
                                    ALU.mult).then_inc(sig_in, 1)
            dve.wait_ge(sig_e, 1)
            link(nc.vector.tensor_scalar(rt[:, 2], rt[:, 1], 1.0, None, ALU.add))
            link(nc.vector.reciprocal(rt[:, 3], rt[:, 2]))
            lower = float(0.5 - np.log(4.0 / 3.0))
            center = float(1.0 / np.e)
            link(nc.vector.tensor_scalar(rt[:, 0], rt[:, 3], -center, None, ALU.add))
            link(nc.vector.tensor_scalar(rt[:, 1], rt[:, 0], -1.0, None, ALU.mult))
            nc.vector.tensor_tensor(rt[:, 4], rt[:, 0], rt[:, 1], ALU.max).then_inc(wexp_in, 1)
            link(nc.vector.tensor_scalar(rt[:, 7], rt[:, 3], lower, None, ALU.is_ge))
            link(nc.vector.tensor_scalar(rt[:, 8], rt[:, 3], 0.5, None, ALU.is_le))
            link(nc.vector.tensor_tensor(rt[:, 7], rt[:, 7], rt[:, 8], ALU.mult))
            dve.wait_ge(wexp, 2)
            link(nc.vector.tensor_tensor(rt[:, 9], rt[:, 5], rt[:, 7], ALU.mult))
            link(nc.vector.tensor_reduce(rs2[:, 0], te(9), AX_X, ALU.add))
            link(nc.vector.tensor_scalar(rs2[:, 1], rs2[:, 0], 1e-8, None, ALU.is_lt))
            link(nc.vector.tensor_scalar(rs2[:, 2], rs2[:, 1], -1.0, 1.0, ALU.mult, ALU.add))
            hidden(0, 0)
            rank_w = rank_sb[:].unsqueeze(1).broadcast_to([P, NT, E])
            values = 6
            for best in (10, 11):
                link(nc.vector.tensor_reduce(rs2[:, 3], te(values), AX_X, ALU.max))
                link(nc.vector.tensor_tensor(te(14), te(values), wide(rs2[:, 3]), ALU.is_equal))
                link(nc.vector.tensor_tensor(te(14), te(14), rank_w, ALU.mult))
                link(nc.vector.tensor_reduce(rs2[:, 4], te(14), AX_X, ALU.max))
                link(nc.vector.tensor_tensor(te(best), te(14), wide(rs2[:, 4]), ALU.is_equal))
                if best == 10:
                    hidden(0, 1)
                    link(nc.vector.scalar_tensor_tensor(rt[:, 13], rt[:, best], 0.0, rt[:, values], ALU.is_equal,
                                                        ALU.mult))
                    values = 13
            hidden(0, 2)
            link(nc.vector.tensor_tensor(rt[:, 11], rt[:, 11], rt[:, 10], ALU.add))
            link(nc.vector.tensor_tensor(rt[:, 11], rt[:, 11], rt[:, 6], ALU.mult))
            link(nc.vector.tensor_reduce(rs2[:, 3], te(11), AX_X, ALU.add))
            link(nc.vector.tensor_scalar(rs2[:, 3], rs2[:, 3], 1e-8, None, ALU.max))
            link(nc.vector.reciprocal(rs2[:, 4], rs2[:, 3]))
            link(nc.vector.tensor_tensor(te(11), te(11), wide(rs2[:, 4]), ALU.mult))
            link(nc.vector.tensor_tensor(te(11), te(11), wide(rs2[:, 1]), ALU.mult))
            link(nc.vector.tensor_tensor(te(9), te(9), wide(rs2[:, 2]), ALU.mult))
            link(nc.vector.tensor_tensor(rt[:, 9], rt[:, 9], rt[:, 11], ALU.add))
            link(nc.vector.tensor_reduce(rs2[:, 5], te(9), AX_X, ALU.add))
            link(nc.vector.tensor_scalar(rs2[:, 5], rs2[:, 5], 1e-8, None, ALU.max))
            link(nc.vector.reciprocal(rs2[:, 6], rs2[:, 5]))
            link(nc.vector.tensor_tensor(te(12), te(9), wide(rs2[:, 6]), ALU.mult))

            def combine(tb, e):
                n = E * tb + e
                dve.wait_ge(down_mm, n + 1)
                if not (isinstance(tb, int) and n < 1):
                    dve.wait_ge(comb_ok, TPB * n)
                for c in range(TPB):
                    t = TPB * tb + c
                    src = ps[:, DOWN[e % len(DOWN)], c * D:(c + 1) * D]
                    tile = slice(t * D, (t + 1) * D) if isinstance(t, int) else bass.ds(t * D, D)
                    w = t * E + e
                    wt = rt[:, 12, w:w + 1] if isinstance(w, int) else rt[:, 12, bass.ds(w, 1)]
                    y = x_flat if e == 0 else o_flat
                    nc.vector.scalar_tensor_tensor(o_flat[:, tile], src, wt, y[:, tile], ALU.mult,
                                                   ALU.add).then_inc(comb_ok, 1)

            hidden(0, 3)
            combined = 0
            for n in range(4, E):
                for _ in range(2):
                    if combined < n - 1:
                        combine(0, combined)
                        combined += 1
                hidden(0, n)
            with dve.Fori(1, NB) as tb:
                for e in range(E):
                    if e < 2:
                        combine(tb - 1, E - 2 + e)
                    else:
                        combine(tb, e - 2)
                    hidden(tb, e)
            combine(NB - 1, E - 2)
            combine(NB - 1, E - 1)

        @block.tensor
        def _(pe):
            mm = nc.tensor.matmul
            pe.wait_ge(id_in, 16)
            pe.wait_ge(silu_ok, 1)
            pe.wait_ge(mod_in, 16)
            for i in range(6):
                mm(ps[:, 7, 2 * D + i:2 * D + i + 1], wmod_sb[:, i * D:(i + 1) * D], cs[:, 4:5], start=True, stop=True)
            for i, g in enumerate((2, 5)):
                last = mm(ps[:, 7, i * D:(i + 1) * D], silu_b[:], wmod_sb[:, g * D:(g + 1) * D], start=True, stop=True)
            last.then_inc(mod_mm, 1)
            for n in range(NB):
                pe.wait_ge(z_ok, (n + 1) * TPB // 2)
                pe.wait_ge(za_ok, (n + 1) * TPB // 2)
                for c in range(TPB):
                    last = nc.tensor.transpose(ps[:, n, c * P:(c + 1) * P], z_sb[:, n * TPB + c, :], id_f[:])
                last.then_inc(zT, 1)
            pe.wait_ge(w_rot, 8)
            pe.wait_ge(ones, 1)
            for i in range(4):
                last = mm(ps[:, 6, i:i + 1], b_row[0:1, i, :], ones_row[0:1, 0:1], start=True, stop=True)
            last.then_inc(col_mm, 1)

            def project_values(n):
                if n >= 2:
                    pe.wait_ge(v_ok, n - 1)
                for c in range(TPB):
                    t = n * TPB + c
                    last = mm(ps[:, 4 + n % 2, c * D:(c + 1) * D], hT[:, t * P:(t + 1) * P], w_sb[:, 4, :],
                              start=True, stop=True)
                last.then_inc(vproj, 1)

            pe.wait_ge(wv_in, 16)
            for i in range(2 * NB):
                qk, n = i // NB, i % NB
                pe.wait_ge(hT_ok, min(2 * i + 2, NB))
                if i >= 2:
                    pe.wait_ge(rope, i - 1)
                for r in range(2):
                    last = mm(ps[:, 2 * (i % 2) + r, :], w_sb[:, 2 * qk + r, :], hT[:, n * BANK:(n + 1) * BANK],
                              start=True, stop=True)
                last.then_inc(proj, 1)
                if i % 2 == 1:
                    project_values(i // 2)

            def score(b, k, j, n, prev):
                pe.wait_ge(m_done, prev)
                mm(ps[:, MB + n % RING, :], m_q[0:SCORE_ROWS, b, k * P:(k + 1) * P],
                   m_k[0:SCORE_ROWS, b, j * BANK:(j + 1) * BANK], start=True, stop=True).then_inc(m_full, 1)

            def shift_transpose(h, read=True):
                pe.wait_ge(m_ready, h + 1)
                if read:
                    pe.wait_ge(ctx_ok, h - 1)
                nc.tensor.transpose(ps[:, AUX, 0:P // 2].bitcast(BF16), m_split[:], id_b[:]).then_inc(mT_mm, 1)

            def sums_transpose(h):
                pe.wait_ge(cx_ok, h + 1)
                pe.wait_ge(mT_ok, h + 2)
                for c in range(TPB):
                    last = nc.tensor.transpose(ps[:, AUX, c * P:(c + 1) * P], cx[:, c * P:(c + 1) * P], id_f[:])
                last.then_inc(cxT, 1)

            pe.wait_ge(pad_ok, 3)
            pe.wait_ge(v_ok, NB)
            pe.wait_ge(rope, 2 * NB)
            pe.wait_ge(id_ok, 1)
            pe.wait_ge(half_in, 2 * SPLITS * 16)
            for i, (m, j) in enumerate(FIRST_MAX):
                if i == EARLY:
                    pe.wait_ge(rest_in, SPLITS * 16)
                if (m, j) == (NT, 0):
                    pe.wait_ge(setm[1], SET)
                if 2 * i >= WIDE:
                    pe.wait_ge(m_done, 2 * i - WIDE + 2)
                for c in range(2):
                    mm(ps[:, (2 * i + PRO_OFF) % WIDE + c, :],
                       m_q[0:SCORE_ROWS, m // NT, m % NT * P:(m % NT + 1) * P],
                       m_k[0:SCORE_ROWS, m // NT, (j + c) * BANK:(j + c + 1) * BANK],
                       start=True, stop=True).then_inc(m_full, 1)
                if (m, j) == (NT, 2):
                    shift_transpose(0, read=False)
            pe.wait_ge(pad_ok, 9)
            pe.wait_ge(m_done, PRO * NB - 2)

            def values(step, k):
                b = (k // NT) % 2
                kt = k % NT
                pe.wait_ge(p_done, (step + 1) * NB)
                for j in range(NB):
                    last = mm(ps[32 * j:32 * j + 32, ACC, :], v_head[:, b, kt, :],
                              probs[:, k % PSLOTS, j * BANK:(j + 1) * BANK], start=(kt == 0), stop=(kt == NT - 1))
                last.then_inc(pv_done, 1)

            def pair(p, first=False, last=False):
                for k in range(PAIR):
                    m = k + PRO
                    b = k // NT
                    if k % NT == 0:
                        pe.wait_ge(sete[b], SET * (p + 1))
                        pe.wait_ge(shift[b], 16 * (p + 1))
                    do_max = not last or m < PAIR
                    if do_max and m % NT == 0:
                        pe.wait_ge(setm[(m // NT) % 2], SET * (p + m // PAIR + (m // NT) % 2))
                    for j in range(NB):
                        q = NB * k + j
                        before = previous(q)
                        if last and q >= LONE + WIDE:
                            before = q - WIDE
                        elif last and q >= LONE:
                            before = LONE - 1
                        if last and q == LONE + RING:
                            pe.wait_ge(m_done, H * NT * NB)
                        if not first or q >= RING:
                            pe.wait_ge(p_done, p * PAIR * NB + before + 1)
                        mm(ps[:, exp_bank(q, last), :], e_k[:, b, (k % NT) * P:(k % NT + 1) * P],
                           e_q[:, b, j * BANK:(j + 1) * BANK], start=True, stop=True).then_inc(s_full, 1)
                        if k % NT == NT - 2 and j == 1 and not (last and b == 1):
                            shift_transpose(2 * p + b + 1, read=not first or b == 1)
                        if do_max:
                            score((m // NT) % 2, m % NT, j, q,
                                  PRO * NB if first and q < RING else (p * PAIR + PRO) * NB + previous(q) + 1)
                    if k == 0:
                        if not first:
                            values(p * PAIR - 1, PAIR - 1)
                    else:
                        if (k - 1) % NT == 0:
                            pe.wait_ge(vh_ok, 2 * p + b + 1)
                            if not first or b == 1:
                                pe.wait_ge(cx_ok, 2 * p + b)
                        values(p * PAIR + k - 1, k - 1)
                    if k % NT == 2 and not (first and k == 2):
                        sums_transpose(2 * p + b - 1)

            pair(0, first=True)
            with pe.Fori(1, H // 2 - 1) as p:
                pair(p)
            pair(H // 2 - 1, last=True)
            values(H * NT - 1, PAIR - 1)
            pe.wait_ge(cx_ok, H)
            pe.wait_ge(ctx_ok, H - 1)
            for cc in range(TPB):
                last = nc.tensor.transpose(ps[:, AUX, cc * P:(cc + 1) * P], cx[:, cc * P:(cc + 1) * P], id_f[:])
            last.then_inc(cxT, 1)

            def second_transpose(n):
                pe.wait_ge(z2_ok, (n + 1) * TPB // 2)
                pe.wait_ge(za2_ok, (n + 1) * TPB // 2)
                if n >= 2:
                    pe.wait_ge(hT2_ok, n - 1)
                for cc in range(TPB):
                    last = nc.tensor.transpose(ps[:, ZT2 + n % 2, cc * P:(cc + 1) * P],
                                                 z_sb[:, n * TPB + cc, :], id_f[:])
                last.then_inc(zT2, 1)

            def logits(n):
                pe.wait_ge(hT2_ok, n + 1)
                for t in range(n * TPB, (n + 1) * TPB):
                    last = mm(ps[:, ACC, t * E:(t + 1) * E], hT[:, t * P:(t + 1) * P], wr_sb[:],
                                start=True, stop=True)
                last.then_inc(log_mm, 1)

            def gate_up(tb, e):
                n = E * tb + e
                first = isinstance(tb, int) and n < 2
                if not first:
                    pe.wait_ge(h_ok, n - 1)
                col = slice(tb * BANK, (tb + 1) * BANK) if isinstance(tb, int) else bass.ds(tb * BANK, BANK)
                mm(ps[:, 2 * (e % 2), :], wg_sb[:, e, :], hT[:, col], start=True, stop=True)
                mm(ps[:, 2 * (e % 2) + 1, :], wu_sb[:, e, :], hT[:, col], start=True, stop=True).then_inc(gu_mm, 1)

            def down(tb, e):
                n = E * tb + e
                pe.wait_ge(h_ok, n + 1)
                if isinstance(tb, int) and n == len(DOWN) - 1:
                    pe.wait_ge(sig_in, 1)
                if not (isinstance(tb, int) and n < len(DOWN)):
                    pe.wait_ge(comb_ok, TPB * (n - len(DOWN) + 1))
                for cc in range(TPB):
                    last = mm(ps[:, DOWN[e % len(DOWN)], cc * D:(cc + 1) * D], hh[e % 2][:, cc * P:(cc + 1) * P],
                                wd_sb[:, e, :], start=True, stop=True)
                last.then_inc(down_mm, 1)

            pe.wait_ge(f_in, 80)
            pe.wait_ge(wd_ok, E)
            for n in range(NB):
                second_transpose(n)
                if n >= 1:
                    logits(n - 1)
            logits(NB - 1)
            gate_up(0, 0)
            for e in range(1, E):
                gate_up(0, e)
                down(0, e - 1)
            with pe.Fori(1, NB) as tb:
                for e in range(E):
                    gate_up(tb, e)
                    if e == 0:
                        down(tb - 1, E - 1)
                    else:
                        down(tb, e - 1)
            down(NB - 1, E - 1)


_INS = ["L0_attn_hidden_states", "L0_attn_Wq", "L0_attn_bq", "L0_attn_Wk", "L0_attn_bk", "L0_attn_Wv", "L0_attn_bv",
        "L0_ffn_Wg", "L0_ffn_Wu", "L0_ffn_Wd", "L0_ffn_Wr", "L0_ffn_temperature", "L0_c", "L0_wmod"]


def tables():
    pos = np.arange(S, dtype=np.float32)
    inv = np.power(10000.0, -2.0 * np.arange(HD // 2) / HD).astype(np.float32)
    ang = (pos[None, :] * np.repeat(inv, 2)[:, None]).astype(np.float32).astype(np.float64)
    cos_t = np.tile(np.cos(ang), (H, 1)).astype(np.float32)
    sin_t = np.tile(np.sin(ang), (H, 1)).astype(np.float32)
    return {"cos": cos_t, "sin": sin_t, "ident": np.eye(P, dtype=np.float32),
            "rank": np.tile(np.arange(E, 0, -1, dtype=np.float32), (P, 1))}


def kernel(**inputs):
    import concourse.bacc as bacc
    from concourse.bass_utils import run_bass_kernel_spmd

    nc = bacc.Bacc("TRN2", target_bir_lowering=False, num_devices=1)
    arrays, args = {}, []
    for name, a in [(n, np.ascontiguousarray(inputs[n])) for n in _INS] + list(tables().items()):
        arrays[f"in_{name}_dram"] = a
        args.append(nc.dram_tensor(f"in_{name}_dram", a.shape, mybir.dt.from_np(a.dtype), kind="ExternalInput").ap())
    args.append(nc.dram_tensor("out_0_dram", (1, S, D), F32, kind="ExternalOutput").ap())
    adaln_block(nc, *args)
    r = run_bass_kernel_spmd(nc, [arrays], core_ids=[0])
    return r.results[0]["out_0_dram"]
```
